# Optimizing a Trainium2 kernel written in Bass

```python
import numpy as np
import jax
import jax.numpy as jnp

def _softmax(x, axis=-1):
    return jax.nn.softmax(x, axis=axis)

def _gelu(x):
    return jax.nn.gelu(x, approximate=True)

def _silu(x):
    return jax.nn.silu(x)

def _sigmoid(x):
    return jax.nn.sigmoid(x)

def _layernorm(x, axis=-1, eps=1e-05):
    m = jnp.mean(x, axis=axis, keepdims=True)
    v = jnp.var(x, axis=axis, keepdims=True)
    return (x - m) / jnp.sqrt(v + eps)

def _scatter_add(tgt, idx, src, axis=0):
    return tgt.at[idx].add(src)

def _segment_sum(src, seg, n):
    return jax.ops.segment_sum(src, seg, n)
kernel_name = 'mk_seq_postln_d1_jaxref_r4_dfec09'

def setup_inputs(seed: int=0):
    np.random.seed(seed)
    _w = jnp.asarray

    def _L0_attn_setup():
        import jax, jax.numpy as jnp
        import numpy as np
        B, T, C = (4, 512, 256)
        NUM_HEADS = 16
        OUT_DIM = 256
        HEAD_DIM = OUT_DIM // NUM_HEADS
        key = jax.random.key(seed)
        kx, kk, kq, kv, kp = jax.random.split(key, 5)
        return {'x': jax.random.normal(kx, (B, T, C), dtype=jnp.float32), 'W_key': jax.random.normal(kk, (OUT_DIM, C), dtype=jnp.float32), 'W_query': jax.random.normal(kq, (OUT_DIM, C), dtype=jnp.float32), 'W_value': jax.random.normal(kv, (OUT_DIM, C), dtype=jnp.float32), 'W_proj': jax.random.normal(kp, (OUT_DIM, OUT_DIM), dtype=jnp.float32)}
    _L0_attn_in = _L0_attn_setup()

    def _L0_ffn_setup():
        import jax, jax.numpy as jnp
        import numpy as np
        DIM = 256
        NUM_EXPERTS = 8
        HIDDEN = 1024
        CAP_FACTOR = 2.0
        B, S = (4, 512)
        key = jax.random.key(seed)
        ks = jax.random.split(key, 6)
        scale_r = 1.0 / np.sqrt(DIM)
        scale_1 = 1.0 / np.sqrt(DIM)
        scale_2 = 1.0 / np.sqrt(HIDDEN)
        return {'x': jax.random.normal(ks[0], (B, S, DIM), dtype=jnp.float32), 'router_w': jax.random.uniform(ks[1], (NUM_EXPERTS, DIM), jnp.float32, -scale_r, scale_r), 'w1': jax.random.uniform(ks[2], (NUM_EXPERTS, DIM, HIDDEN), jnp.float32, -scale_1, scale_1), 'b1': jax.random.uniform(ks[3], (NUM_EXPERTS, HIDDEN), jnp.float32, -scale_1, scale_1), 'w2': jax.random.uniform(ks[4], (NUM_EXPERTS, HIDDEN, DIM), jnp.float32, -scale_2, scale_2), 'b2': jax.random.uniform(ks[5], (NUM_EXPERTS, DIM), jnp.float32, -scale_2, scale_2)}
    _L0_ffn_in = _L0_ffn_setup()
    _d = {'L0_attn_x': _L0_attn_in['x'], 'L0_attn_W_key': _L0_attn_in['W_key'], 'L0_attn_W_query': _L0_attn_in['W_query'], 'L0_attn_W_value': _L0_attn_in['W_value'], 'L0_attn_W_proj': _L0_attn_in['W_proj'], 'L0_ffn_router_w': _L0_ffn_in['router_w'], 'L0_ffn_w1': _L0_ffn_in['w1'], 'L0_ffn_b1': _L0_ffn_in['b1'], 'L0_ffn_w2': _L0_ffn_in['w2'], 'L0_ffn_b2': _L0_ffn_in['b2']}
    _x0 = _d['L0_attn_x']
    _d['L0_attn_x'] = jax.random.normal(jax.random.fold_in(jax.random.key(seed), 1), (8, 512, 256), dtype=_x0.dtype)
    del _x0
    return _d

def reference(L0_attn_x, L0_attn_W_key, L0_attn_W_query, L0_attn_W_value, L0_attn_W_proj, L0_ffn_router_w, L0_ffn_w1, L0_ffn_b1, L0_ffn_w2, L0_ffn_b2):

    def _L0_attn_ref(x, W_key, W_query, W_value, W_proj):
        import jax, jax.numpy as jnp
        import numpy as np
        B, T, C = (4, 512, 256)
        NUM_HEADS = 16
        OUT_DIM = 256
        HEAD_DIM = OUT_DIM // NUM_HEADS
        b, t, c = x.shape
        h, hd = (NUM_HEADS, HEAD_DIM)
        inv_sqrt_c = c ** (-0.5)

        def proj(W):
            return jnp.einsum('btc,oc->bto', x, W).reshape(b, t, h, hd).transpose(0, 2, 1, 3) * inv_sqrt_c
        k = proj(W_key)
        q = proj(W_query)
        v = proj(W_value)
        scores = jnp.einsum('bhqd,bhkd->bhqk', q, k) * hd ** (-0.5)
        causal = jnp.tril(jnp.ones((t, t), dtype=bool))
        scores = jnp.where(causal, scores, -jnp.inf)
        weight = jax.nn.softmax(scores, axis=-1)
        out = jnp.einsum('bhqk,bhkd->bhqd', weight, v)
        out = out.transpose(0, 2, 1, 3).reshape(b, t, h * hd)
        out = jnp.einsum('bto,po->btp', out, W_proj) * W_proj.shape[-1] ** (-0.5)
        return out

    def _L0_ffn_ref(x, router_w, w1, b1, w2, b2):
        import jax, jax.numpy as jnp
        import numpy as np
        DIM = 256
        NUM_EXPERTS = 8
        HIDDEN = 1024
        CAP_FACTOR = 2.0
        B, S = (4, 512)
        Bz, Sz, Dz = x.shape
        E = router_w.shape[0]
        capacity = max(1, int(Sz * CAP_FACTOR / E) + 1)
        scores = jax.nn.softmax(jnp.einsum('bsd,ed->bse', x, router_w), axis=-1)
        scores_t = jnp.swapaxes(scores, 1, 2)
        gate_vals, sel_idx = jax.lax.top_k(scores_t, capacity)
        b_idx = jnp.arange(Bz)[:, None, None]
        tokens = x[b_idx, sel_idx]
        h = jnp.einsum('becd,edh->bech', tokens, w1) + b1[None, :, None, :]
        h = jax.nn.gelu(h, approximate=False)
        y = jnp.einsum('bech,ehd->becd', h, w2) + b2[None, :, None, :]
        gated = y * gate_vals[..., None]
        out = jnp.zeros_like(x).at[b_idx, sel_idx].add(gated)
        return out
    x = L0_attn_x
    x = _layernorm(x + _L0_attn_ref(x, L0_attn_W_key, L0_attn_W_query, L0_attn_W_value, L0_attn_W_proj), axis=-1)
    x = _layernorm(x + _L0_ffn_ref(x, L0_ffn_router_w, L0_ffn_w1, L0_ffn_b1, L0_ffn_w2, L0_ffn_b2), axis=-1)
    return x

_drawn_inputs = setup_inputs


def setup_inputs(seed=0):
    import zlib

    import numpy as np

    out = dict(_drawn_inputs(seed))
    spreads = {}
    factors = {'L0_ffn_b1': 8.0, 'L0_ffn_b2': 8.0}
    for name, (base, spread) in spreads.items():
        noise = np.random.default_rng([zlib.crc32(name.encode()), seed]).standard_normal(out[name].shape)
        drawn = base * np.exp(spread * noise) if base else spread * noise
        out[name] = jnp.asarray(drawn.astype(out[name].dtype))
    for name, factor in factors.items():
        out[name] = (out[name] * factor).astype(out[name].dtype)
    return out
```

```python
import numpy as np
import concourse.bass as bass
from concourse import mybir
from contextlib import ExitStack

F32 = mybir.dt.float32
F32R = mybir.dt.float32r
BF16 = mybir.dt.bfloat16
I32 = mybir.dt.int32
U32 = mybir.dt.uint32
ALU = mybir.AluOpType
ACT = mybir.ActivationFunctionType
AX = mybir.AxisListType

P = 128
B, T, C = 8, 512, 256
H, D = 16, 16
E, HID = 8, 1024
CAP = int(T * 2.0 / E) + 1
KC = C // P
TT = T // P
KH = HID // P
PAIRS = H // 2
GROUPS = H // 4
VW = 32
BIG_NEG = -1.0e30
EPS = 1e-5
S_SCALE = float(C) ** -1 * float(D) ** -0.5
O_SCALE = float(C) ** -0.5 * float(C) ** -0.5

K_PARTS = (0, 0, 1, 1, 0, 2)
Q_PARTS = (0, 1, 0, 1, 2, 0)
K_RUNS = ((0, 2, 0, 0), (2, 2, 1, 0), (4, 2, 0, 2))
Q_RUNS = ((0, 2, 0, 1), (2, 2, 0, 1), (4, 1, 2, 0), (5, 1, 0, 0))
KQ = len(K_PARTS) * D
KM = KQ + 3

ST_UNITS = (((0, 0, 0),), ((0, 1, 0), (0, 3, 384)), ((0, 2, 0), (1, 2, 256)), ((1, 0, 0),), ((1, 1, 0), (1, 3, 384)))
UP = len(ST_UNITS)
ST_AT = {(h, kb): (u, c) for u, unit in enumerate(ST_UNITS) for h, kb, c in unit}
N_UNITS = [u for h0 in (0, H // 2) for u in
           [(3, h0 + h, 1) for h in range(8)] + [(2, h0 + h, 1) for h in range(8)] +
           [(1, h0 + h, 2) for h in range(0, 8, 2)] + [(0, h0 + h, 4) for h in range(0, 8, 4)]]
NU = len(N_UNITS)
N_QUARTER = NU // 4
ST_RING, N_RING, PT_RING = 3, 2, 4

STAGES = (
    (0, 0, "res", 0, 0), (0, 0, "stack", 1, 1), (0, 2, "qk", 2, 0), (0, 6, "qk", 2, 1), (0, 8, "onorm", -1, 2),
    (1, 1, "onorm", -1, 3), (1, 3, "ot", -1, 0), (1, 4, "ot", -1, 1), (1, 6, "qk", 2, 2), (1, 8, "proj", -1, 0),
    (1, 9, "proj", -1, 1),
    (2, 0, "stack", 2, 0), (2, 1, "onorm", 0, 0), (2, 2, "qk", 2, 3), (2, 4, "v", 2, 0), (2, 6, "x1", -1, 0),
    (2, 7, "v", 2, 1), (2, 9, "x1t", -1, 0),
    (3, 0, "nmcut", 1, 0), (3, 1, "onorm", 0, 1), (3, 2, "nm", 1, 0), (3, 3, "x1t", -1, 1), (3, 5, "logit", -1, 0), (3, 7, "split", 3, 0),
    (3, 9, "score", -1, 0),
)
AV_PLACES = (4, 5, 6, 7)
BY_ACT = ("qk", "v", "nm", "ot", "x1t")
BY_DVE = ("onorm", "proj", "logit")


def steps():
    for i in range(-3, B + 1):
        for g in range(4):
            nat_b, nat_0 = (i + 2, 0) if g == 3 else (i + 1, (g + 1) * N_QUARTER)
            for k in range(10):
                if 0 <= i < B:
                    yield "st", i, (2 * g) * UP + k
                if 0 <= nat_b < B:
                    for n in range(N_QUARTER * k // 10, N_QUARTER * (k + 1) // 10):
                        yield "nat", nat_b, nat_0 + n
                group = i * GROUPS + g - 1
                if k in AV_PLACES and 0 <= group < B * GROUPS:
                    yield "av", group, AV_PLACES.index(k)
                for gg, kk, stage, ahead, n in STAGES:
                    if (gg, kk) == (g, k) and 0 <= i + ahead < B:
                        yield stage, i + ahead, n


def numbers(stages):
    return {x: n for n, x in enumerate(x for x in steps() if x[0] in stages)}


def attention(nc, ctx, xt_d, x_d, wqkv_d, wp_d, rw_d, x1_d, acc_d, ident, scores):
    def sb(name, shape, dt):
        return ctx.enter_context(nc.sbuf_tensor(name, shape, dt))

    def pb(name, shape, dt=F32):
        return ctx.enter_context(nc.psum_tensor(name, shape, dt))

    def sem(name):
        return ctx.enter_context(nc.semaphore(name))

    w_hi = sb("w_hi", [P, KC, 3 * C], F32R)
    w_lo = sb("w_lo", [P, KC, 3 * C], F32R)
    wp = sb("wp", [P, KC, C], F32)
    rw = sb("rw", [P, KC, E], F32)
    ident_b = sb("ident_b", [P, P], BF16)
    tri = sb("tri", [P, 4, P], BF16)
    xt = sb("xt", [P, KC, T], F32)
    xt_hi = sb("xt_hi", [P, KC, T], F32R)
    xt_lo = sb("xt_lo", [P, KC, T], F32R)
    qk_f = sb("qk_f", [P, 2, T], F32)
    qk_r = sb("qk_r", [P, T], F32)
    parts = sb("parts", [P, 2, 3, T], BF16)
    kst = sb("kst", [KM, 2, H, T], BF16)
    qst = sb("qst", [KM, 2, H, T], BF16)
    vaug = sb("vaug", [P, 3, TT, H, VW], F32)
    nmax = sb("nmax", [P, 2, TT, H], F32)
    nmax_r = sb("nmax_r", [P, TT, H], F32)
    nm3 = sb("nm3", [P, TT, 3, H], BF16)
    nmt = sb("nmt", [3 * H, T], BF16)
    pt = sb("pt", [P, PT_RING, UP, T], F32)
    av_sb = sb("av_sb", [P, 2, T], F32)
    rden = sb("rden", [P, TT, 4], F32)
    o_nat = sb("o_nat", [P, TT, C], F32)
    o_t = sb("o_t", [P, KC, T], F32)
    res = sb("res", [P, 2, TT, C], F32)
    stats = sb("stats", [P, TT, 6], F32)
    mv = sb("mv", [P, TT, 2], F32)
    ve = sb("ve", [P, TT], F32)
    half = sb("half", [P, TT], F32)
    rstd = sb("rstd", [P, TT], F32)
    x1t = sb("x1t", [P, KC, T], F32)
    lg = sb("lg", [P, TT, E], F32)
    lge = sb("lge", [P, TT, E], F32)
    lmax = sb("lmax", [P, TT], F32)
    lsum = sb("lsum", [P, TT], F32)
    linv = sb("linv", [P, TT], F32)

    st_ps = [pb(f"st_ps{n}", [P, T]) for n in range(ST_RING)]
    n_ps = [pb(f"n_ps{n}", [P, T]) for n in range(N_RING)]
    av_ps = pb("av_ps", [P, T])
    act_ps = pb("act_ps", [P, T])
    dve_ps = pb("dve_ps", [P, T])
    nm_ps = act_ps[:, :].bitcast(BF16)

    w_in = sem("w_in")
    w_split = sem("w_split")
    pool_step = sem("pool_step")
    consts = sem("consts")
    dve_step = sem("dve_step")
    xt_in = sem("xt_in")
    x_hi = sem("x_hi")
    x_split = sem("x_split")
    res_in = [sem("res_in0"), sem("res_in1")]
    qk_first = sem("qk_first")
    qk_rest = sem("qk_rest")
    parts_out = [sem("parts_out0"), sem("parts_out1")]
    stack_in = [[sem(f"stack{h}{p}") for p in range(2)] for h in range(2)]
    nat_done = sem("nat_done")
    max_done = sem("max_done")
    nm_parts = sem("nm_parts")
    rows_in = sem("rows_in")
    st_done = sem("st_done")
    exp_done = sem("exp_done")
    masked = sem("masked")
    av_done = sem("av_done")
    av_out = sem("av_out")
    act_ready = sem("act_ready")
    act_free = sem("act_free")
    dve_ready = sem("dve_ready")
    dve_free = sem("dve_free")
    var_ready = sem("var_ready")
    rstd_ready = sem("rstd_ready")
    x1_ready = sem("x1_ready")
    x1_out = sem("x1_out")
    lexp = sem("lexp")
    scored = sem("scored")

    part_d = nc.dram_tensor("part_d", [2, 2, 3, D, H, T], BF16).ap()

    act_no, dve_no = numbers(BY_ACT), numbers(BY_DVE)

    block = ctx.enter_context(nc.Block())

    @block.sync
    def _(sp):
        def load_xt(b):
            sp.dma_start(xt[:, :, :], xt_d[:, b * T:(b + 1) * T].rearrange("(k p) n -> p k n", p=P)).then_inc(xt_in, 16)

        load_xt(0)
        sp.dma_start(pt[:, 0, 0:3, :], wqkv_d.rearrange("(k p) n -> p k n", p=P)).then_inc(w_in, 16)
        sp.dma_start(wp[:, :, :], wp_d.rearrange("(k p) n -> p k n", p=P)).then_inc(w_in, 16)
        sp.dma_start(rw[:, :, :], rw_d.rearrange("(k p) n -> p k n", p=P)).then_inc(w_in, 16)
        for stage, b, n in steps():
            if stage == "split" and b + 1 < B:
                sp.wait_ge(x_split, b + 1)
                load_xt(b + 1)
            elif stage == "res":
                if b >= 2:
                    sp.wait_ge(x1_out, 32 * (b - 1))
                    sp.wait_ge(act_ready, act_no[("x1t", b - 2, 1)] + 1)
                sp.dma_start(res[:, b % 2, :, :], x_d[b * T:(b + 1) * T, :].rearrange("(t p) n -> p t n", p=P)).then_inc(res_in[b % 2], 16)
            elif stage == "qk":
                tile, which, half_ = 4 * b + n, n % 2, n // 2
                sp.wait_ge(qk_first, tile + 1)
                sp.wait_ge(qk_rest, tile + 1)
                if b >= 2:
                    sp.wait_ge(stack_in[half_][b % 2], 16 * (len(K_RUNS) + len(Q_RUNS)) * (b // 2))
                for part in range(3):
                    dst = part_d[which, b % 2, part, :, 8 * half_:8 * half_ + 8, :]
                    sp.dma_start(dst.rearrange("d h n -> h d n"), parts[:, tile % 2, part, :]).then_inc(parts_out[tile % 2], 16)
            elif stage == "stack":
                for parity in range(2):
                    sp.wait_ge(parts_out[parity], 48 * (2 * b + n + 1))
                if b >= 2:
                    sp.wait_ge(st_done, ((b - 2) * PAIRS + 4 * (n + 1)) * UP)
                for which, stack, runs in ((0, qst, Q_RUNS), (1, kst, K_RUNS)):
                    for at, count, first, step in runs:
                        src = part_d[which, b % 2, first:first + 1 + step * (count - 1):max(step, 1), :, 8 * n:8 * n + 8, :]
                        if step == 0:
                            src = src.to_broadcast([count, D, 8, T])
                        sp.dma_start(stack[at * D:(at + count) * D, b % 2, 8 * n:8 * n + 8, :],
                                     src.rearrange("i d h n -> i d (h n)")).then_inc(stack_in[n][b % 2], 16)
            elif stage == "nm":
                sp.wait_ge(act_free, act_no[(stage, b, n)] + 1)
                for at in range(3):
                    sp.dma_start(qst[KQ + at:KQ + at + 1, b % 2, :, :], nmt[at * H:(at + 1) * H, :]).then_inc(rows_in, 16)
            elif stage == "x1":
                sp.wait_ge(x1_ready, TT * (b + 1))
                for dst in (x1_d, acc_d):
                    sp.dma_start(dst[b * T:(b + 1) * T, :].rearrange("(t p) n -> p t n", p=P), res[:, b % 2, :, :]).then_inc(x1_out, 16)
        sp.wait_ge(x1_out, 32 * B)

    @block.gpsimd
    def _(pool):
        made = [0]

        def link(ins):
            made[0] += 1
            ins.then_inc(pool_step, 1)
            pool.wait_ge(pool_step, made[0])

        link(nc.gpsimd.memset(ident[:, :], 0.0))
        link(nc.gpsimd.affine_select(out=ident[:, :], in_=ident[:, :], compare_op=ALU.not_equal, fill=1.0, base=0,
                                     pattern=[[-1, P]], channel_multiplier=1))
        nc.gpsimd.tensor_copy(ident_b[:, :], ident[:, :]).then_inc(consts, 1)
        link(nc.gpsimd.memset(tri[:, :, :], 0.0))
        nc.gpsimd.affine_select(out=tri[:, :, :], in_=tri[:, :, :], compare_op=ALU.is_ge, fill=BIG_NEG, base=0,
                                pattern=[[0, 4], [-1, P]], channel_multiplier=1).then_inc(consts, 1)
        link(nc.gpsimd.memset(half[:, :], -0.5))
        two_ones = float(np.array([0x3F803F80], np.uint32).view(np.float32)[0])
        nc.gpsimd.memset(kst[KQ:KM, :, :, :].rearrange("p a h n -> p (a h n)").bitcast(F32), two_ones).then_inc(consts, 1)
        pool.wait_ge(consts, 3)
        link(nc.gpsimd.memset(vaug[:, :, :, :, D:VW], 0.0))
        nc.gpsimd.memset(vaug[:, :, :, :, D:D + 1], 1.0).then_inc(consts, 1)

        for stage, b, n in steps():
            if stage == "st":
                pool.wait_ge(exp_done, (b * PAIRS * UP) + n + 1)
                pair, u = n // UP, n % UP
                tiles = [c // P for _, _, c in ST_UNITS[u]]
                x = pt[:, (b * PAIRS + pair) % PT_RING, u, :].rearrange("p (j q) -> p j q", q=P)
                x = x[:, tiles[0]:tiles[-1] + 1:max(1, tiles[-1] - tiles[0]), :]
                nc.gpsimd.affine_select(out=x, in_=x, compare_op=ALU.is_ge, fill=0.0, base=0,
                                        pattern=[[0, len(tiles)], [1, P]], channel_multiplier=-1).then_inc(masked, 1)
            elif stage == "qk":
                tile = 4 * b + n
                pool.wait_ge(qk_first, tile + 1)
                pool.wait_ge(act_free, act_no[(stage, b, n)] + 1)
                if tile:
                    pool.wait_ge(qk_rest, tile)
                if tile >= 2:
                    pool.wait_ge(parts_out[tile % 2], 48 * (tile // 2))
                link(nc.gpsimd.tensor_tensor(qk_r[:, :], qk_f[:, tile % 2, :], parts[:, tile % 2, 0, :], ALU.subtract))
                link(nc.gpsimd.tensor_tensor(parts[:, tile % 2, 1, :], qk_f[:, tile % 2, :], parts[:, tile % 2, 0, :], ALU.subtract))
                nc.gpsimd.tensor_tensor(parts[:, tile % 2, 2, :], qk_r[:, :], parts[:, tile % 2, 1, :], ALU.subtract).then_inc(qk_rest, 1)
            elif stage == "split":
                pool.wait_ge(x_hi, b + 1)
                nc.gpsimd.tensor_tensor(xt_lo[:, :, :], xt[:, :, :], xt_hi[:, :, :].bitcast(F32), ALU.subtract).then_inc(x_split, 1)
            elif stage == "x1":
                pool.wait_ge(var_ready, b + 1)
                nc.gpsimd.tensor_tensor(rstd[:, :], ve[:, :], half[:, :], ALU.pow).then_inc(rstd_ready, 1)

    @block.scalar
    def _(act):
        for stage, b, n in steps():
            if stage in BY_ACT:
                act.wait_ge(act_ready, act_no[(stage, b, n)] + 1)
            if stage == "st":
                at, slot = b * PAIRS * UP + n, b * PAIRS + n // UP
                act.wait_ge(st_done, at + 1)
                if n % UP == 0 and slot >= PT_RING:
                    act.wait_ge(av_done, (slot - PT_RING) // 2 + 1)
                nc.scalar.activation(pt[:, slot % PT_RING, n % UP, :], st_ps[at % ST_RING][:, :], ACT.Exp,
                                     scale=S_SCALE).then_inc(exp_done, 1)
            elif stage == "split":
                act.wait_ge(xt_in, 16 * (b + 1))
                if b >= 1:
                    act.wait_ge(act_ready, act_no[("v", b - 1, 1)] + 1)
                    act.wait_ge(x_split, b)
                nc.scalar.activation(xt_hi[:, :, :], xt[:, :, :], ACT.Copy).then_inc(x_hi, 1)
            elif stage == "av" and n == 3:
                act.wait_ge(av_done, b + 1)
                if b >= 2:
                    last = ("onorm", (b - 2) // GROUPS, (b - 2) % GROUPS)
                    act.wait_ge(dve_ready, dve_no[last] + 1)
                nc.scalar.activation(av_sb[:, b % 2, :], av_ps[:, :], ACT.Copy).then_inc(av_out, 1)
            elif stage == "qk":
                tile = 4 * b + n
                if tile >= 2:
                    act.wait_ge(qk_rest, tile - 1)
                    act.wait_ge(parts_out[tile % 2], 48 * (tile // 2))
                nc.scalar.activation(parts[:, tile % 2, 0, :], act_ps[:, :], ACT.Copy).then_inc(qk_first, 1)
                nc.scalar.activation(qk_f[:, tile % 2, :], act_ps[:, :], ACT.Copy).then_inc(act_free, 1)
            elif stage == "v":
                if b == 0 and n == 0:
                    act.wait_ge(consts, 4)
                if b >= 3:
                    act.wait_ge(av_done, (b - 2) * GROUPS)
                src = act_ps[:, :].rearrange("p (t h d) -> p t h d", t=2, h=H)
                for t in range(2):
                    ins = nc.scalar.activation(vaug[:, b % 3, 2 * n + t, :, 0:D], src[:, t, :, :], ACT.Copy)
                ins.then_inc(act_free, 1)
            elif stage == "nm":
                if b >= 1:
                    act.wait_ge(rows_in, 48 * b)
                nc.scalar.activation(nmt[:, :], nm_ps[0:3 * H, 0:T], ACT.Copy).then_inc(act_free, 1)
            elif stage == "ot":
                if b >= 1:
                    act.wait_ge(dve_ready, dve_no[("proj", b - 1, 1)] + 1)
                nc.scalar.activation(o_t[:, n, :], act_ps[:, :], ACT.Copy).then_inc(act_free, 1)
            elif stage == "x1t":
                if b >= 1:
                    act.wait_ge(dve_ready, dve_no[("logit", b - 1, 0)] + 1)
                nc.scalar.activation(x1t[:, n, :], act_ps[:, :], ACT.Copy).then_inc(act_free, 1)
            elif stage == "logit":
                act.wait_ge(dve_free, dve_no[(stage, b, n)] + 1)
                if b >= 1:
                    act.wait_ge(scored, b)
                nc.scalar.activation(lge[:, :, :], lg[:, :, :], ACT.Exp).then_inc(lexp, 1)

    @block.vector
    def _(dve):
        made = [0]

        def link(ins):
            made[0] += 1
            ins.then_inc(dve_step, 1)
            dve.wait_ge(dve_step, made[0])

        dve.wait_ge(w_in, 48)
        raw = pt[:, 0, 0:3, :].rearrange("p a n -> p (a n)").rearrange("p (k n) -> p k n", k=KC)
        link(nc.vector.tensor_copy(w_hi[:, :, :], raw))
        nc.vector.tensor_tensor(w_lo[:, :, :], raw, w_hi[:, :, :].bitcast(F32), ALU.subtract).then_inc(w_split, 1)
        for stage, b, n in steps():
            if stage in BY_DVE:
                dve.wait_ge(dve_ready, dve_no[(stage, b, n)] + 1)
            if stage == "nat":
                qb, h0, heads = N_UNITS[n]
                at = b * NU + n
                dve.wait_ge(nat_done, at + 1)
                src = n_ps[at % N_RING][:, 0:heads * (qb + 1) * P].rearrange("p (h k) -> p h k", h=heads)
                nc.vector.tensor_reduce(out=nmax[:, b % 2, qb, h0:h0 + heads], in_=src, axis=AX.X, op=ALU.max, negate=True).then_inc(max_done, 1)
            elif stage == "nmcut":
                dve.wait_ge(max_done, NU * (b + 1))
                if b >= 1:
                    dve.wait_ge(act_ready, act_no[("nm", b - 1, 0)] + 1)
                link(nc.vector.tensor_copy(nm3[:, :, 0, :], nmax[:, b % 2, :, :]))
                link(nc.vector.tensor_tensor(nmax_r[:, :, :], nmax[:, b % 2, :, :], nm3[:, :, 0, :], ALU.subtract))
                link(nc.vector.tensor_copy(nm3[:, :, 1, :], nmax_r[:, :, :]))
                nc.vector.tensor_tensor(nm3[:, :, 2, :], nmax_r[:, :, :], nm3[:, :, 1, :], ALU.subtract).then_inc(nm_parts, 1)
            elif stage == "onorm":
                src = dve_ps[:, :].rearrange("p (t j v) -> p t j v", t=TT, j=4)
                link(nc.vector.reciprocal(rden[:, :, :], src[:, :, :, D]))
                if b >= 1 and n == 0:
                    dve.wait_ge(act_ready, act_no[("ot", b - 1, 1)] + 1)
                dst = o_nat[:, :, 4 * D * n:4 * D * (n + 1)].rearrange("p t (j d) -> p t j d", j=4)
                nc.vector.tensor_tensor(dst, src[:, :, :, 0:D], rden[:, :, :].unsqueeze(3).to_broadcast([P, TT, 4, D]), ALU.mult).then_inc(dve_free, 1)
            elif stage == "proj":
                if n == 0:
                    dve.wait_ge(res_in[b % 2], 16 * (b // 2 + 1))
                rows = res[:, b % 2, 2 * n:2 * n + 2, :].rearrange("p t c -> p (t c)")
                nc.vector.scalar_tensor_tensor(out=rows, in0=dve_ps[:, :], scalar=O_SCALE, in1=rows,
                                               op0=ALU.mult, op1=ALU.add).then_inc(dve_free, 1)
                dve.wait_ge(dve_free, dve_no[(stage, b, n)] + 1)
                for t in (2 * n, 2 * n + 1):
                    ins = nc.vector.bn_stats(stats[:, t, :], res[:, b % 2, t, :])
                    if t % 2 == 0:
                        ins.then_inc(dve_step, 1)
                        made[0] += 1
                link(ins)
                for t in (2 * n, 2 * n + 1):
                    ins = nc.vector.bn_aggr(mv[:, t, :], stats[:, t, :])
                    if t % 2 == 0:
                        ins.then_inc(dve_step, 1)
                        made[0] += 1
                link(ins)
                if n == 1:
                    nc.vector.tensor_scalar_add(ve[:, :], mv[:, :, 1], EPS).then_inc(var_ready, 1)
            elif stage == "x1":
                dve.wait_ge(rstd_ready, b + 1)
                for t in range(TT):
                    row = res[:, b % 2, t, :]
                    nc.vector.tensor_scalar(row, row, mv[:, t, 0:1], rstd[:, t:t + 1], ALU.subtract, ALU.mult).then_inc(x1_ready, 1)
            elif stage == "logit":
                src = dve_ps[:, 0:TT * E].rearrange("p (t e) -> p t e", t=TT)
                link(nc.vector.tensor_reduce(out=lmax[:, :], in_=src, axis=AX.X, op=ALU.max))
                if b >= 1:
                    dve.wait_ge(lexp, b)
                nc.vector.tensor_tensor(lg[:, :, :], src, lmax[:, :].unsqueeze(2).to_broadcast([P, TT, E]), ALU.subtract).then_inc(dve_free, 1)
            elif stage == "score":
                dve.wait_ge(lexp, b + 1)
                link(nc.vector.tensor_reduce(out=lsum[:, :], in_=lge[:, :, :], axis=AX.X, op=ALU.add))
                link(nc.vector.reciprocal(linv[:, :], lsum[:, :]))
                nc.vector.tensor_tensor(scores[:, :, b, :], lge[:, :, :], linv[:, :].unsqueeze(2).to_broadcast([P, TT, E]), ALU.mult).then_inc(scored, 1)

    @block.tensor
    def _(pe):
        pe.wait_ge(consts, 4)
        pe.wait_ge(w_in, 48)
        pe.wait_ge(w_split, 1)
        for stage, b, n in steps():
            if stage in BY_ACT and act_no[(stage, b, n)]:
                pe.wait_ge(act_free, act_no[(stage, b, n)])
            if stage in BY_DVE and dve_no[(stage, b, n)]:
                pe.wait_ge(dve_free, dve_no[(stage, b, n)])
            if stage == "st":
                at = b * PAIRS * UP + n
                pair, u = n // UP, n % UP
                if n == 0:
                    pe.wait_ge(rows_in, 48 * (b + 1))
                if at >= ST_RING:
                    pe.wait_ge(exp_done, at - ST_RING + 1)
                for hh, kb, c in ST_UNITS[u]:
                    h = 2 * pair + hh
                    ins = nc.tensor.matmul(st_ps[at % ST_RING][:, c:c + T - kb * P], kst[0:KM, b % 2, h, kb * P:(kb + 1) * P],
                                           qst[0:KM, b % 2, h, kb * P:T], start=True, stop=True)
                ins.then_inc(st_done, 1)
            elif stage == "nat":
                qb, h0, heads = N_UNITS[n]
                at = b * NU + n
                if n % (NU // 2) == 0:
                    pe.wait_ge(stack_in[n // (NU // 2)][b % 2], 16 * (len(K_RUNS) + len(Q_RUNS)) * (b // 2 + 1))
                if at >= N_RING:
                    pe.wait_ge(max_done, at - N_RING + 1)
                bank, w = n_ps[at % N_RING], (qb + 1) * P
                if qb == 0:
                    nc.tensor.matmul(bank[:, :], ident_b[:, :], tri[:, :, :].rearrange("p a k -> p (a k)"), start=True, stop=False)
                for j in range(heads):
                    h = h0 + j
                    ins = nc.tensor.matmul(bank[:, j * w:(j + 1) * w], qst[0:KQ, b % 2, h, qb * P:(qb + 1) * P],
                                           kst[0:KQ, b % 2, h, 0:w], start=qb > 0, stop=qb > 0 or j == heads - 1)
                    if qb > 0:
                        ins = nc.tensor.matmul(bank[:, (j + 1) * w - P:(j + 1) * w], ident_b[:, :], tri[:, 0, :], start=False, stop=True,
                                               skip_group_check=True)
                ins.then_inc(nat_done, 1)
            elif stage == "av":
                seq, group = b // GROUPS, b % GROUPS
                if n == 0:
                    pe.wait_ge(masked, (2 * b + 2) * UP)
                    if b:
                        pe.wait_ge(av_out, b)
                    if group == 0:
                        pe.wait_ge(act_free, act_no[("v", seq, 1)] + 1)
                for j in range(4):
                    h = 4 * group + j
                    u, c = ST_AT[(h % 2, n)]
                    ins = nc.tensor.matmul(av_ps[VW * j:VW * (j + 1), n * P:T], vaug[:, seq % 3, n, h, :],
                                           pt[:, (seq * PAIRS + h // 2) % PT_RING, u, c:c + T - n * P], start=n == 0, stop=n == TT - 1,
                                           skip_group_check=True)
                if n == TT - 1:
                    ins.then_inc(av_done, 1)
            elif stage == "onorm":
                group = b * GROUPS + n
                pe.wait_ge(av_out, group + 1)
                for t in range(TT):
                    ins = nc.tensor.transpose(dve_ps[:, t * P:(t + 1) * P], av_sb[:, group % 2, t * P:(t + 1) * P], ident[:, :])
                ins.then_inc(dve_ready, 1)
            elif stage == "qk":
                which, half_ = n % 2, n // 2
                pe.wait_ge(x_split, b + 1)
                cols = slice(which * C + half_ * P, which * C + half_ * P + P)
                for at, (w, x) in enumerate(((w_hi, xt_hi), (w_hi, xt_lo), (w_lo, xt_hi))):
                    for k in range(KC):
                        ins = nc.tensor.matmul(act_ps[:, :], w[:, k, cols], x[:, k, :], start=at + k == 0, stop=at == 2 and k == KC - 1)
                ins.then_inc(act_ready, 1)
            elif stage == "v":
                for t in range(2):
                    toks = slice((2 * n + t) * P, (2 * n + t + 1) * P)
                    for at, (w, x) in enumerate(((w_hi, xt_hi), (w_hi, xt_lo), (w_lo, xt_hi))):
                        for k in range(KC):
                            ins = nc.tensor.matmul(act_ps[:, t * C:(t + 1) * C], x[:, k, toks], w[:, k, 2 * C:3 * C],
                                                   start=at + k == 0, stop=at == 2 and k == KC - 1)
                ins.then_inc(act_ready, 1)
            elif stage == "nm":
                pe.wait_ge(nm_parts, b + 1)
                for t in range(TT):
                    ins = nc.tensor.transpose(nm_ps[0:3 * H, t * P:(t + 1) * P], nm3[:, t, :, :].rearrange("p i h -> p (i h)"), ident_b[:, :])
                ins.then_inc(act_ready, 1)
            elif stage == "ot":
                pe.wait_ge(dve_free, dve_no[("onorm", b, 3)] + 1)
                for t in range(TT):
                    ins = nc.tensor.transpose(act_ps[:, t * P:(t + 1) * P], o_nat[:, t, n * P:(n + 1) * P], ident[:, :])
                ins.then_inc(act_ready, 1)
            elif stage == "proj":
                pe.wait_ge(act_free, act_no[("ot", b, 1)] + 1)
                for t in range(2):
                    toks = slice((2 * n + t) * P, (2 * n + t + 1) * P)
                    for k in range(KC):
                        ins = nc.tensor.matmul(dve_ps[:, t * C:(t + 1) * C], o_t[:, k, toks], wp[:, k, :], start=k == 0, stop=k == KC - 1)
                ins.then_inc(dve_ready, 1)
            elif stage == "x1t":
                pe.wait_ge(x1_ready, TT * (b + 1))
                for t in range(TT):
                    ins = nc.tensor.transpose(act_ps[:, t * P:(t + 1) * P], res[:, b % 2, t, n * P:(n + 1) * P], ident[:, :])
                ins.then_inc(act_ready, 1)
            elif stage == "logit":
                pe.wait_ge(act_free, act_no[("x1t", b, 1)] + 1)
                for t in range(TT):
                    for k in range(KC):
                        ins = nc.tensor.matmul(dve_ps[:, t * E:(t + 1) * E], x1t[:, k, t * P:(t + 1) * P], rw[:, k, :],
                                               start=k == 0, stop=k == KC - 1)
                ins.then_inc(dve_ready, 1)


LEFT = B
CHUNKS = ((0, 1, LEFT), (2, 3, 4), (5, 6, 7))
NQ = E * len(CHUNKS)
ROUNDS = -(-CAP // 8)
H_RING, Y_RING, TOK_RING, G_RING = 3, 3, 3, 3


def chunk(q):
    tiles = CHUNKS[q % len(CHUNKS)]
    return q // len(CHUNKS), tiles, sum(rows_of(j) for j in tiles)


def rows_of(tile):
    return B if tile == LEFT else P


def expert_steps():
    yield "turn", 0, 0
    yield "turn", 1, 0
    for m in range(KH):
        yield "up", 0, m
    for q in range(NQ):
        for m in range(KH + 1):
            if q + 1 < NQ and m < KH:
                yield "up", q + 1, m
            if m == 1 and q % 3 == 0 and q // 3 + 1 < E:
                yield "cut1", q // 3 + 1, 0
            if m == 1 and q % 3 == 1 and q // 3 + 1 < E:
                yield "cut2", q // 3 + 1, 0
            if m == 4 and q + 2 < NQ:
                yield "turn", q + 2, 0
            if m in (2, 5, 8):
                yield "down", q, m // 3


def experts(nc, ctx, x1_d, acc_d, w1_d, b1_d, w2_d, b2_d, out_d, ident, scores):
    def sb(name, shape, dt):
        return ctx.enter_context(nc.sbuf_tensor(name, shape, dt))

    def sem(name):
        return ctx.enter_context(nc.semaphore(name))

    R = B * E
    pool_s = [sb(f"pool_s{n}", [R, T], F32) for n in range(2)]
    vals = sb("vals", [R, 8 * ROUNDS], F32)
    idx = sb("idx", [R, 8 * ROUNDS], U32)
    idx_f = sb("idx_f", [R, 8 * ROUNDS], F32)
    base_i = sb("base_i", [P, B, E], I32)
    lbase_i = sb("lbase_i", [B, E], I32)
    tok_no = sb("tok_no", [P, B, E], U32)
    gate = sb("gate", [P, B, E], F32)
    left_f = sb("left_f", [B, E], F32)
    left_no = sb("left_no", [B, E], U32)
    left_gate = sb("left_gate", [B, E], F32)
    b1 = sb("b1", [P, E, KH], F32)
    b2 = sb("b2", [P, E, C], F32)
    w1_raw = sb("w1_raw", [P, KC, HID], F32)
    w2_raw = sb("w2_raw", [P, KH, C], F32)
    w1_hi = sb("w1_hi", [P, 2, KC, HID], F32R)
    w1_lo = sb("w1_lo", [P, 2, KC, HID], F32R)
    w2_hi = sb("w2_hi", [P, 2, KH, C], F32R)
    w2_lo = sb("w2_lo", [P, 2, KH, C], F32R)
    tok = sb("tok", [P, TOK_RING, 3, C], F32)
    tt_hi = sb("tt_hi", [P, TOK_RING, KC, 3 * P], F32R)
    tt_lo = sb("tt_lo", [P, TOK_RING, KC, 3 * P], F32R)
    g = sb("g", [P, G_RING, 3 * P], F32)
    h_hi = sb("h_hi", [P, 2, KH, 3 * P], F32R)
    h_lo = sb("h_lo", [P, 2, KH, 3 * P], F32R)
    y = sb("y", [P, B + 1, C], F32)
    fin = sb("fin", [P, 2, TT, C], F32)
    stats2 = sb("stats2", [P, TT, 6], F32)
    mv2 = sb("mv2", [P, 2, TT, 2], F32)
    ve2 = sb("ve2", [P, 2, TT], F32)
    half2 = sb("half2", [P, TT], F32)
    rstd2 = sb("rstd2", [P, 2, TT], F32)

    h_ps = [ctx.enter_context(nc.psum_tensor(f"h_ps{n}", [P, T], F32)) for n in range(H_RING)]
    y_ps = [ctx.enter_context(nc.psum_tensor(f"y_ps{n}", [P, T], F32)) for n in range(Y_RING)]
    tp_ps = [ctx.enter_context(nc.psum_tensor(f"tp_ps{n}", [P, T], F32)) for n in range(KC)]

    sel_t = sem("sel_t")
    sel_step = sem("sel_step")
    bases = sem("bases")
    sel_f = sem("sel_f")
    left_in = sem("left_in")
    sel_done = sem("sel_done")
    bias_in = sem("bias_in")
    w1_in, w2_in = sem("w1_in"), sem("w2_in")
    w1_cut, w2_cut = sem("w1_cut"), sem("w2_cut")
    tok_in = [sem(f"tok_in{n}") for n in range(TOK_RING)]
    tp_done = sem("tp_done")
    tp_hi = sem("tp_hi")
    tp_lo = sem("tp_lo")
    h_done = sem("h_done")
    g_done = sem("g_done")
    g_hi, g_lo = sem("g_hi"), sem("g_lo")
    y_done = sem("y_done")
    y_out = sem("y_out")
    y_ready = sem("y_ready")
    added = [sem(f"added{n}") for n in range(B + 1)]
    fin_in = [sem(f"fin_in{n}") for n in range(2)]
    fin_step = sem("fin_step")
    fin_var, fin_rstd, fin_done = sem("fin_var"), sem("fin_rstd"), sem("fin_done")
    fin_out = [sem(f"fin_out{n}") for n in range(2)]

    block = ctx.enter_context(nc.Block())

    @block.sync
    def _(sp):
        def load_w1(e):
            sp.dma_start(w1_raw[:, :, :], w1_d[e].rearrange("(k p) n -> p k n", p=P)).then_inc(w1_in, 16)

        def load_w2(e):
            sp.dma_start(w2_raw[:, :, :], w2_d[e].rearrange("(k p) n -> p k n", p=P)).then_inc(w2_in, 16)

        load_w1(0)
        load_w2(0)
        sp.dma_start(b1[:, :, :], b1_d.rearrange("p (e m) -> p e m", e=E)).then_inc(bias_in, 16)
        sp.dma_start(b2[:, :, :], b2_d.rearrange("e c -> (e c)").rearrange("(o n) -> o n", o=1).to_broadcast([P, E * C])).then_inc(bias_in, 16)
        sp.wait_ge(w1_cut, 2)
        load_w1(1)
        sp.wait_ge(w2_cut, 2)
        load_w2(1)
        sp.wait_ge(sel_f, 1)
        sp.dma_start(left_f[:, :], idx_f[:, P:P + 1]).then_inc(left_in, 16)
        sp.dma_start(left_gate[:, :], vals[:, P:P + 1]).then_inc(left_in, 16)
        for stage, q, n in expert_steps():
            if stage == "cut1" and q + 1 < E:
                sp.wait_ge(w1_cut, 2 * (q + 1))
                load_w1(q + 1)
            elif stage == "cut2" and q + 1 < E:
                sp.wait_ge(w2_cut, 2 * (q + 1))
                load_w2(q + 1)

        def store(b):
            sp.wait_ge(fin_done, TT * (b + 1))
            sp.dma_start(out_d[b * T:(b + 1) * T, :].rearrange("(t p) n -> p t n", p=P), fin[:, b % 2, :, :]).then_inc(fin_out[b % 2], 16)

        for b in range(B):
            sp.wait_ge(added[b], 16 * E)
            sp.wait_ge(added[LEFT], 16 * E)
            if b >= 2:
                sp.wait_ge(fin_out[b % 2], 16 * (b // 2))
            sp.dma_start(fin[:, b % 2, :, :], acc_d[b * T:(b + 1) * T, :].rearrange("(t p) n -> p t n", p=P)).then_inc(fin_in[b % 2], 16)
            if b:
                store(b - 1)
        store(B - 1)
        for n in range(2):
            sp.wait_ge(fin_out[n], 16 * B // 2)

    @block.gpsimd
    def _(pool):
        nc.gpsimd.iota(base_i[:, :, :], pattern=[[T, B], [0, E]], base=0, channel_multiplier=0).then_inc(bases, 1)
        nc.gpsimd.iota(lbase_i[:, :], pattern=[[0, E]], base=0, channel_multiplier=T).then_inc(bases, 1)
        nc.gpsimd.memset(half2[:, :], -0.5).then_inc(bases, 1)
        pool.wait_ge(sel_done, 4)

        def choice(e, j):
            return left_no[:, e:e + 1] if j == LEFT else tok_no[:, j, e:e + 1]

        def gather(q):
            e, tiles, _ = chunk(q)
            if q >= TOK_RING:
                pool.wait_ge(tp_done, KC * (q - TOK_RING + 1))
            for at, j in enumerate(tiles):
                nc.gpsimd.indirect_dma_start(tok[0:rows_of(j), q % TOK_RING, at, :], None, x1_d[:, :],
                                             bass.IndirectOffsetOnAxis(ap=choice(e, j), axis=0)).then_inc(tok_in[q % TOK_RING], 16)

        for q in range(TOK_RING):
            gather(q)
        for stage, q, n in expert_steps():
            if stage == "turn" and TOK_RING <= q + 1 < NQ:
                gather(q + 1)
            elif stage == "down":
                e, tiles, _ = chunk(q)
                j = tiles[n]
                pool.wait_ge(y_ready, 3 * q + n + 1)
                if e:
                    for other in (range(B + 1) if j == LEFT else (j, LEFT)):
                        pool.wait_ge(added[other], 16 * e)
                nc.gpsimd.indirect_dma_start(acc_d[:, :], bass.IndirectOffsetOnAxis(ap=choice(e, j), axis=0),
                                             y[0:rows_of(j), j, :], None, compute_op=ALU.add).then_inc(added[j], 16)
        pool.wait_ge(bases, 3)
        for b in range(B):
            pool.wait_ge(fin_var, b + 1)
            nc.gpsimd.tensor_tensor(rstd2[:, b % 2, :], ve2[:, b % 2, :], half2[:, :], ALU.pow).then_inc(fin_rstd, 1)

    @block.scalar
    def _(act):
        act.wait_ge(bias_in, 32)
        for stage, q, n in expert_steps():
            if stage == "turn":
                _, _, cols = chunk(q)
                for k in range(KC):
                    act.wait_ge(tp_done, KC * q + k + 1)
                    if q >= TOK_RING:
                        act.wait_ge(h_done, KH * (q - TOK_RING + 1))
                    nc.scalar.activation(tt_hi[:, q % TOK_RING, k, 0:cols], tp_ps[k][:, 0:cols], ACT.Copy).then_inc(tp_hi, 1)
            elif stage == "up":
                e, _, cols = chunk(q)
                at = KH * q + n
                act.wait_ge(h_done, at + 1)
                if at >= G_RING:
                    act.wait_ge(g_lo, at - G_RING + 1)
                nc.scalar.activation(g[:, at % G_RING, 0:cols], h_ps[at % H_RING][:, 0:cols], ACT.Gelu,
                                     bias=b1[:, e, n:n + 1]).then_inc(g_done, 1)

    @block.vector
    def _(dve):
        made = [0]

        def link(ins):
            made[0] += 1
            ins.then_inc(sel_step, 1)
            dve.wait_ge(sel_step, made[0])

        def cut(raw, hi, lo, ready):
            nc.vector.tensor_copy(hi, raw).then_inc(ready, 1)

        dve.wait_ge(sel_t, 1)
        link(nc.vector.tensor_copy(pool_s[0][:, :], y_ps[0][0:R, :]))
        for r in range(ROUNDS):
            src, best = pool_s[r % 2], slice(8 * r, 8 * r + 8)
            link(nc.vector.max(vals[:, best], src[:, :]))
            nc.vector.max_index(idx[:, best], vals[:, best], src[:, :]).then_inc(sel_step, 1)
            made[0] += 1
            if r + 1 < ROUNDS:
                link(nc.vector.match_replace(pool_s[(r + 1) % 2][:, :], vals[:, best], src[:, :], -1.0))
        dve.wait_ge(sel_step, made[0])
        nc.vector.tensor_copy(idx_f[:, :], idx[:, :]).then_inc(sel_f, 1)
        dve.wait_ge(w1_in, 16)
        nc.vector.tensor_copy(w1_hi[:, 0, :, :], w1_raw[:, :, :]).then_inc(w1_cut, 1)
        dve.wait_ge(w1_cut, 1)
        nc.vector.tensor_tensor(w1_lo[:, 0, :, :], w1_raw[:, :, :], w1_hi[:, 0, :, :].bitcast(F32), ALU.subtract).then_inc(w1_cut, 1)
        dve.wait_ge(w2_in, 16)
        nc.vector.tensor_copy(w2_hi[:, 0, :, :], w2_raw[:, :, :]).then_inc(w2_cut, 1)
        dve.wait_ge(w2_cut, 1)
        nc.vector.tensor_tensor(w2_lo[:, 0, :, :], w2_raw[:, :, :], w2_hi[:, 0, :, :].bitcast(F32), ALU.subtract).then_inc(w2_cut, 1)
        dve.wait_ge(sel_t, 3)
        dve.wait_ge(bases, 3)
        nc.vector.tensor_tensor(tok_no[:, :, :], y_ps[1][:, 0:R].rearrange("p (b e) -> p b e", b=B), base_i[:, :, :], ALU.add).then_inc(sel_done, 1)
        nc.vector.tensor_copy(gate[:, :, :], y_ps[2][:, 0:R].rearrange("p (b e) -> p b e", b=B)).then_inc(sel_done, 1)
        dve.wait_ge(left_in, 32)
        nc.vector.tensor_tensor(left_no[:, :], left_f[:, :], lbase_i[:, :], ALU.add).then_inc(sel_done, 2)
        dve.wait_ge(bias_in, 32)
        for stage, q, n in expert_steps():
            if stage == "turn":
                _, _, cols = chunk(q)
                for k in range(KC):
                    dve.wait_ge(tp_hi, KC * q + k + 1)
                    nc.vector.tensor_tensor(tt_lo[:, q % TOK_RING, k, 0:cols], tp_ps[k][:, 0:cols],
                                            tt_hi[:, q % TOK_RING, k, 0:cols].bitcast(F32), ALU.subtract).then_inc(tp_lo, 1)
            elif stage == "up":
                _, _, cols = chunk(q)
                at = KH * q + n
                dve.wait_ge(g_done, at + 1)
                if q >= 2 and n == 0:
                    dve.wait_ge(y_done, 3 * (q - 1))
                hi = h_hi[:, q % 2, n, 0:cols]
                nc.vector.tensor_copy(hi, g[:, at % G_RING, 0:cols]).then_inc(g_hi, 1)
                dve.wait_ge(g_hi, at + 1)
                nc.vector.tensor_tensor(h_lo[:, q % 2, n, 0:cols], g[:, at % G_RING, 0:cols], hi.bitcast(F32), ALU.subtract).then_inc(g_lo, 1)
            elif stage == "down":
                e, tiles, _ = chunk(q)
                j, at = tiles[n], 3 * q + n
                rows = rows_of(j)
                dve.wait_ge(y_done, at + 1)
                if e:
                    dve.wait_ge(added[j], 16 * e)
                nc.vector.tensor_tensor(y[0:rows, j, :], y_ps[at % Y_RING][0:rows, 0:C], b2[0:rows, e, :], ALU.add).then_inc(y_out, 1)
                dve.wait_ge(y_out, at + 1)
                by = left_gate[:, e:e + 1] if j == LEFT else gate[:, j, e:e + 1]
                nc.vector.tensor_scalar(y[0:rows, j, :], y[0:rows, j, :], by, None, ALU.mult).then_inc(y_ready, 1)
            elif stage in ("cut1", "cut2"):
                raw, hi, lo, came, done = ((w1_raw, w1_hi, w1_lo, w1_in, w1_cut) if stage == "cut1" else
                                           (w2_raw, w2_hi, w2_lo, w2_in, w2_cut))
                if q >= 2:
                    dve.wait_ge(y_done, 3 * 3 * (q - 1))
                dve.wait_ge(came, 16 * (q + 1))
                nc.vector.tensor_copy(hi[:, q % 2, :, :], raw[:, :, :]).then_inc(done, 1)
                dve.wait_ge(done, 2 * q + 1)
                nc.vector.tensor_tensor(lo[:, q % 2, :, :], raw[:, :, :], hi[:, q % 2, :, :].bitcast(F32), ALU.subtract).then_inc(done, 1)
        for b in range(B):
            dve.wait_ge(fin_in[b % 2], 16 * (b // 2 + 1))
            for t in range(TT):
                nc.vector.bn_stats(stats2[:, t, :], fin[:, b % 2, t, :]).then_inc(fin_step, 1)
            dve.wait_ge(fin_step, 2 * TT * b + TT)
            for t in range(TT):
                nc.vector.bn_aggr(mv2[:, b % 2, t, :], stats2[:, t, :]).then_inc(fin_step, 1)
            dve.wait_ge(fin_step, 2 * TT * (b + 1))
            nc.vector.tensor_scalar_add(ve2[:, b % 2, :], mv2[:, b % 2, :, 1], EPS).then_inc(fin_var, 1)
            dve.wait_ge(fin_rstd, b + 1)
            for t in range(TT):
                row = fin[:, b % 2, t, :]
                nc.vector.tensor_scalar(row, row, mv2[:, b % 2, t, 0:1], rstd2[:, b % 2, t:t + 1], ALU.subtract, ALU.mult).then_inc(fin_done, 1)

    @block.tensor
    def _(pe):
        for t in range(TT):
            ins = nc.tensor.transpose(y_ps[0][0:R, t * P:(t + 1) * P], scores[:, t, :, :].rearrange("p b e -> p (b e)"), ident[:, :])
        ins.then_inc(sel_t, 1)
        pe.wait_ge(sel_f, 1)
        nc.tensor.transpose(y_ps[1][:, 0:R], idx_f[:, 0:P], ident[0:R, 0:R]).then_inc(sel_t, 1)
        nc.tensor.transpose(y_ps[2][:, 0:R], vals[:, 0:P], ident[0:R, 0:R]).then_inc(sel_t, 1)
        pe.wait_ge(sel_done, 4)
        for stage, q, n in expert_steps():
            e, tiles, cols = chunk(q) if stage in ("turn", "up", "down") else (0, (), 0)
            if stage == "turn":
                pe.wait_ge(tok_in[q % TOK_RING], 48 * (q // TOK_RING + 1))
                for k in range(KC):
                    if q:
                        pe.wait_ge(tp_lo, KC * (q - 1) + k + 1)
                    for at, j in enumerate(tiles):
                        rows = rows_of(j)
                        ins = nc.tensor.transpose(tp_ps[k][:, at * P:at * P + rows], tok[0:rows, q % TOK_RING, at, k * P:(k + 1) * P],
                                                  ident[0:rows, 0:rows])
                    ins.then_inc(tp_done, 1)
            elif stage == "up":
                at = KH * q + n
                if n == 0:
                    pe.wait_ge(tp_hi, KC * (q + 1))
                    pe.wait_ge(tp_lo, KC * (q + 1))
                    pe.wait_ge(w1_cut, 2 * (e + 1))
                if at >= H_RING:
                    pe.wait_ge(g_done, at - H_RING + 1)
                units = slice(n * P, (n + 1) * P)
                terms = [(w, x, k) for w, x in ((w1_hi, tt_hi), (w1_hi, tt_lo), (w1_lo, tt_hi)) for k in range(KC)]
                for i, (w, x, k) in enumerate(terms):
                    ins = nc.tensor.matmul(h_ps[at % H_RING][:, 0:cols], w[:, e % 2, k, units], x[:, q % TOK_RING, k, 0:cols],
                                           start=i == 0, stop=i == len(terms) - 1)
                ins.then_inc(h_done, 1)
            elif stage == "down":
                at, rows = 3 * q + n, rows_of(tiles[n])
                if n == 0:
                    pe.wait_ge(g_hi, KH * (q + 1))
                    pe.wait_ge(g_lo, KH * (q + 1))
                    pe.wait_ge(w2_cut, 2 * (e + 1))
                if at >= Y_RING:
                    pe.wait_ge(y_out, at - Y_RING + 1)
                toks = slice(n * P, n * P + rows)
                terms = [(x, w, m) for m in range(KH) for x, w in ((h_hi, w2_hi), (h_lo, w2_hi), (h_hi, w2_lo))]
                for i, (x, w, m) in enumerate(terms):
                    ins = nc.tensor.matmul(y_ps[at % Y_RING][0:rows, 0:C], x[:, q % 2, m, toks], w[:, e % 2, m, :],
                                           start=i == 0, stop=i == len(terms) - 1)
                ins.then_inc(y_done, 1)


def build(nc, xt_d, x_d, wqkv_d, wp_d, rw_d, w1_d, b1_d, w2_d, b2_d, out_d):
    x1_d = nc.dram_tensor("x1", [B * T, C], F32).ap()
    acc_d = nc.dram_tensor("acc", [B * T, C], F32).ap()
    with ExitStack() as both:
        ident = both.enter_context(nc.sbuf_tensor("ident", [P, P], F32))
        scores = both.enter_context(nc.sbuf_tensor("scores", [P, TT, B, E], F32))
        with ExitStack() as ctx:
            attention(nc, ctx, xt_d, x_d, wqkv_d, wp_d, rw_d, x1_d, acc_d, ident, scores)
        with ExitStack() as ctx:
            experts(nc, ctx, x1_d, acc_d, w1_d, b1_d, w2_d, b2_d, out_d, ident, scores)


def kernel(L0_attn_x, L0_attn_W_key, L0_attn_W_query, L0_attn_W_value, L0_attn_W_proj,
           L0_ffn_router_w, L0_ffn_w1, L0_ffn_b1, L0_ffn_w2, L0_ffn_b2):
    import concourse.bacc as bacc
    from concourse.bass_utils import run_bass_kernel_spmd

    x = np.asarray(L0_attn_x).reshape(B * T, C)
    wqkv = np.concatenate([np.asarray(L0_attn_W_query).T, np.asarray(L0_attn_W_key).T, np.asarray(L0_attn_W_value).T], axis=1)
    arrays = {
        "in_xt": x.T,
        "in_x": x,
        "in_wqkv": wqkv,
        "in_wp": np.asarray(L0_attn_W_proj).T,
        "in_rw": np.asarray(L0_ffn_router_w).T,
        "in_w1": np.asarray(L0_ffn_w1),
        "in_b1": np.asarray(L0_ffn_b1).reshape(E, KH, P).transpose(2, 0, 1).reshape(P, E * KH),
        "in_w2": np.asarray(L0_ffn_w2),
        "in_b2": np.asarray(L0_ffn_b2),
    }
    arrays = {n: np.ascontiguousarray(a) for n, a in arrays.items()}
    nc = bacc.Bacc("TRN2", target_bir_lowering=False, num_devices=1)
    args = [nc.dram_tensor(n, a.shape, mybir.dt.from_np(a.dtype), kind="ExternalInput").ap() for n, a in arrays.items()]
    out = nc.dram_tensor("out_0", (B * T, C), F32, kind="ExternalOutput").ap()
    build(nc, *args, out)
    r = run_bass_kernel_spmd(nc, [arrays], core_ids=[0])
    return r.results[0]["out_0"].reshape(B, T, C)
```

```python
import numpy as np
import concourse.bass as bass
from concourse import mybir
from contextlib import ExitStack

F32 = mybir.dt.float32
F32R = mybir.dt.float32r
BF16 = mybir.dt.bfloat16
I32 = mybir.dt.int32
U32 = mybir.dt.uint32
ALU = mybir.AluOpType
ACT = mybir.ActivationFunctionType
AX = mybir.AxisListType

P = 128
B, T, C = 8, 512, 256
H, D = 16, 16
E, HID = 8, 1024
CAP = int(T * 2.0 / E) + 1
KC = C // P
TT = T // P
KH = HID // P
PAIRS = H // 2
GROUPS = H // 4
VW = 32
BIG_NEG = -1.0e30
EPS = 1e-5
S_SCALE = float(C) ** -1 * float(D) ** -0.5
O_SCALE = float(C) ** -0.5 * float(C) ** -0.5

K_PARTS = (0, 0, 1, 1, 0, 2)
Q_PARTS = (0, 1, 0, 1, 2, 0)
K_RUNS = ((0, 2, 0, 0), (2, 2, 1, 0), (4, 2, 0, 2))
Q_RUNS = ((0, 2, 0, 1), (2, 2, 0, 1), (4, 1, 2, 0), (5, 1, 0, 0))
KQ = len(K_PARTS) * D
KM = KQ + 3

ST_UNITS = (((0, 0, 0),), ((0, 1, 0), (0, 3, 384)), ((0, 2, 0), (1, 2, 256)), ((1, 0, 0),), ((1, 1, 0), (1, 3, 384)))
UP = len(ST_UNITS)
ST_AT = {(h, kb): (u, c) for u, unit in enumerate(ST_UNITS) for h, kb, c in unit}
N_UNITS = [u for h0 in (0, H // 2) for u in
           [(3, h0 + h, 1) for h in range(8)] + [(2, h0 + h, 1) for h in range(8)] +
           [(1, h0 + h, 2) for h in range(0, 8, 2)] + [(0, h0 + h, 4) for h in range(0, 8, 4)]]
NU = len(N_UNITS)
N_QUARTER = NU // 4
ST_RING, N_RING, PT_RING = 2, 3, 4

STAGES = (
    (0, 0, "res", 0, 0), (0, 0, "stack", 1, 1), (0, 2, "qk", 2, 0), (0, 6, "qk", 2, 1), (0, 8, "onorm", -1, 2),
    (1, 1, "onorm", -1, 3), (1, 3, "ot", -1, 0), (1, 4, "ot", -1, 1), (1, 6, "qk", 2, 2), (1, 8, "proj", -1, 0),
    (1, 9, "proj", -1, 1),
    (2, 0, "stack", 2, 0), (2, 1, "onorm", 0, 0), (2, 2, "qk", 2, 3), (2, 4, "v", 2, 0), (2, 6, "x1", -1, 0),
    (2, 7, "v", 2, 1), (2, 9, "x1t", -1, 0),
    (3, 0, "nmcut", 1, 0), (3, 1, "onorm", 0, 1), (3, 2, "nm", 1, 0), (3, 3, "x1t", -1, 1), (3, 5, "logit", -1, 0), (3, 7, "split", 3, 0),
    (3, 9, "score", -1, 0),
)
EARLY = 6
ROUNDS = -(-CAP // 8)
ROUND_AT = [(B - 1, 2 + 3 * n) for n in range(13)] + [(B, n) for n in (1, 9, 12, 14)]
STARTED = [(-2, stage, n) for stage in ("qk", "v", "stack") for n in range(4)]
AV_PLACES = (4, 5, 6, 7)
BY_ACT = ("qk", "v", "nm", "ot", "x1t")
BY_DVE = ("onorm", "proj", "logit", "pick", "picked")


def steps():
    for i in range(-3, B + 1):
        for g in range(4):
            nat_b, nat_0 = (i + 2, 0) if g == 3 else (i + 1, (g + 1) * N_QUARTER)
            for k in range(10):
                if 0 <= i < B:
                    yield "st", i, (2 * g) * UP + k
                if 0 <= nat_b < B:
                    for n in range(N_QUARTER * k // 10, N_QUARTER * (k + 1) // 10):
                        yield "nat", nat_b, nat_0 + n
                group = i * GROUPS + g - 1
                if k in AV_PLACES and 0 <= group < B * GROUPS:
                    yield "av", group, AV_PLACES.index(k)
                if (i, g, k) == (-2, 0, 0):
                    for stage, n in (("qk", 0), ("qk", 1), ("stack", 0), ("v", 0), ("qk", 2), ("qk", 3), ("v", 1)):
                        yield stage, 0, n
                for gg, kk, stage, ahead, n in STAGES:
                    if (gg, kk) == (g, k) and 0 <= i + ahead < B and (i, stage, n) not in STARTED:
                        yield stage, i + ahead, n
                place = 10 * g + k
                if (i, place) == (B - 1, 1):
                    yield "pick", 0, 0
                if (i, place) in ROUND_AT:
                    yield "round", 0, ROUND_AT.index((i, place))
                if (i, place) == (B, 16):
                    yield "picked", 0, 0
                    yield "fetch", 0, 0


def numbers(stages):
    return {x: n for n, x in enumerate(x for x in steps() if x[0] in stages)}


def pick_round(nc, link, pool, best, at, r):
    src, eight = pool[r % 2], slice(8 * r, 8 * r + 8)
    link(nc.vector.max(best[:, eight], src[:, :]))
    link(nc.vector.max_index(at[:, eight], best[:, eight], src[:, :]))
    if r + 1 < ROUNDS:
        link(nc.vector.match_replace(pool[(r + 1) % 2][:, :], best[:, eight], src[:, :], -1.0))


def attention(nc, ctx, xt_d, x_d, wqkv_d, wp_d, rw_d, x1_d, acc_d, ident, scores, chosen, w1_d, w2_d, ahead):
    def sb(name, shape, dt):
        return ctx.enter_context(nc.sbuf_tensor(name, shape, dt))

    def pb(name, shape, dt=F32):
        return ctx.enter_context(nc.psum_tensor(name, shape, dt))

    def sem(name):
        return ctx.enter_context(nc.semaphore(name))

    w_hi = sb("w_hi", [P, KC, 3 * C], F32R)
    w_lo = sb("w_lo", [P, KC, 3 * C], F32R)
    wp = sb("wp", [P, KC, C], F32)
    rw = sb("rw", [P, KC, E], F32)
    ident_b = sb("ident_b", [P, P], BF16)
    tri = sb("tri", [P, 4, P], BF16)
    xt = ahead["w1_raw"][:, 0, :].rearrange("p (k n) -> p k n", k=KC)
    qk_f = ahead["w1_raw"][:, 1, :].rearrange("p (a n) -> p a n", a=2)
    w2_flat = ahead["w2_raw"][:, :, :].rearrange("p m c -> p (m c)")
    parts = w2_flat[:, 0:3 * T].bitcast(BF16).rearrange("p (a i n) -> p a i n", a=2, i=3)
    qk_r = w2_flat[:, 3 * T:4 * T]
    xt_hi = sb("xt_hi", [P, KC, T], F32R)
    xt_lo = sb("xt_lo", [P, KC, T], F32R)
    kst = sb("kst", [KM, 2, H, T], BF16)
    qst = sb("qst", [KM, 2, H, T], BF16)
    vaug = sb("vaug", [P, 3, TT, H, VW], F32)
    nmax = sb("nmax", [P, 2, TT, H], F32)
    nmax_r = sb("nmax_r", [P, TT, H], F32)
    nm3 = sb("nm3", [P, TT, 3, H], BF16)
    nmt = sb("nmt", [3 * H, T], BF16)
    pt = sb("pt", [P, PT_RING, UP, T], F32)
    av_sb = sb("av_sb", [P, 2, T], F32)
    rden = sb("rden", [P, TT, 4], F32)
    o_nat = sb("o_nat", [P, TT, C], F32)
    o_t = sb("o_t", [P, KC, T], F32)
    res = sb("res", [P, 2, TT, C], F32)
    stats = sb("stats", [P, TT, 6], F32)
    mv = sb("mv", [P, TT, 2], F32)
    ve = sb("ve", [P, TT], F32)
    half = sb("half", [P, TT], F32)
    rstd = sb("rstd", [P, TT], F32)
    x1t = sb("x1t", [P, KC, T], F32)
    lg = sb("lg", [P, TT, E], F32)
    lge = sb("lge", [P, TT, E], F32)
    lmax = sb("lmax", [P, TT], F32)
    lsum = sb("lsum", [P, TT], F32)
    linv = sb("linv", [P, TT], F32)

    st_ps = [pb(f"st_ps{n}", [P, T]) for n in range(ST_RING)]
    n_ps = [pb(f"n_ps{n}", [P, T]) for n in range(N_RING)]
    av_ps = pb("av_ps", [P, T])
    act_ps = pb("act_ps", [P, T])
    dve_ps = pb("dve_ps", [P, T])
    nm_ps = act_ps[:, :].bitcast(BF16)

    early = EARLY * E
    row_pool = [sb(f"row_pool{n}", [early, T], F32) for n in range(2)]
    best = sb("best", [early, 8 * ROUNDS], F32)
    best_at = sb("best_at", [early, 8 * ROUNDS], U32)
    best_f = sb("best_f", [early, 8 * ROUNDS], F32)
    base_i = sb("base_i", [P, EARLY], I32)

    w_in = sem("w_in")
    wp_in = sem("wp_in")
    w_split = sem("w_split")
    pool_step = sem("pool_step")
    consts = sem("consts")
    dve_step = sem("dve_step")
    xt_in = sem("xt_in")
    x_hi = sem("x_hi")
    x_split = sem("x_split")
    res_in = [sem("res_in0"), sem("res_in1")]
    qk_first = sem("qk_first")
    qk_rest = sem("qk_rest")
    parts_out = [sem("parts_out0"), sem("parts_out1")]
    stack_in = [[sem(f"stack{h}{p}") for p in range(2)] for h in range(2)]
    nat_done = sem("nat_done")
    max_done = sem("max_done")
    nm_parts = sem("nm_parts")
    rows_in = sem("rows_in")
    st_done = sem("st_done")
    exp_done = sem("exp_done")
    masked = sem("masked")
    av_done = sem("av_done")
    av_out = sem("av_out")
    act_ready = sem("act_ready")
    act_free = sem("act_free")
    dve_ready = sem("dve_ready")
    dve_free = sem("dve_free")
    var_ready = sem("var_ready")
    rstd_ready = sem("rstd_ready")
    x1_ready = sem("x1_ready")
    x1_out = sem("x1_out")
    lexp = sem("lexp")
    scored = sem("scored")

    best_ready = sem("best_ready")
    left_in = sem("left_in")
    bases = sem("bases")

    part_d = nc.dram_tensor("part_d", [2, 2, 3, D, H, T], BF16).ap()

    act_no, dve_no = numbers(BY_ACT), numbers(BY_DVE)

    def act_banks(stage, b):
        return ST_RING if stage in ("qk", "v") and b == 0 else 1

    def act_bank(stage, b, n):
        return st_ps[act_no[(stage, b, n)] % ST_RING] if act_banks(stage, b) > 1 else act_ps

    block = ctx.enter_context(nc.Block())

    @block.sync
    def _(sp):
        def load_xt(b):
            sp.dma_start(xt[:, :, :], xt_d[:, b * T:(b + 1) * T].rearrange("(k p) n -> p k n", p=P)).then_inc(xt_in, 16)

        sp.dma_start(pt[:, 0, 0:3, :], wqkv_d.rearrange("(k p) n -> p k n", p=P)).then_inc(w_in, 16)
        load_xt(0)
        sp.dma_start(wp[:, :, :], wp_d.rearrange("(k p) n -> p k n", p=P)).then_inc(wp_in, 16)
        sp.dma_start(rw[:, :, :], rw_d.rearrange("(k p) n -> p k n", p=P)).then_inc(wp_in, 16)
        for stage, b, n in steps():
            if stage == "split" and b + 1 < B:
                sp.wait_ge(x_split, b + 1)
                load_xt(b + 1)
            elif stage == "res":
                if b >= 2:
                    sp.wait_ge(x1_out, 32 * (b - 1))
                    sp.wait_ge(act_ready, act_no[("x1t", b - 2, 1)] + 1)
                sp.dma_start(res[:, b % 2, :, :], x_d[b * T:(b + 1) * T, :].rearrange("(t p) n -> p t n", p=P)).then_inc(res_in[b % 2], 16)
            elif stage == "qk":
                tile, which, half_ = 4 * b + n, n % 2, n // 2
                sp.wait_ge(qk_first, tile + 1)
                sp.wait_ge(qk_rest, tile + 1)
                if b >= 2:
                    sp.wait_ge(stack_in[half_][b % 2], 16 * (len(K_RUNS) + len(Q_RUNS)) * (b // 2))
                for part in range(3):
                    dst = part_d[which, b % 2, part, :, 8 * half_:8 * half_ + 8, :]
                    sp.dma_start(dst.rearrange("d h n -> h d n"), parts[:, tile % 2, part, :]).then_inc(parts_out[tile % 2], 16)
            elif stage == "stack":
                for parity in range(2):
                    sp.wait_ge(parts_out[parity], 48 * (2 * b + n + 1))
                if b >= 2:
                    sp.wait_ge(st_done, ((b - 2) * PAIRS + 4 * (n + 1)) * UP)
                for which, stack, runs in ((0, qst, Q_RUNS), (1, kst, K_RUNS)):
                    for at, count, first, step in runs:
                        src = part_d[which, b % 2, first:first + 1 + step * (count - 1):max(step, 1), :, 8 * n:8 * n + 8, :]
                        if step == 0:
                            src = src.to_broadcast([count, D, 8, T])
                        sp.dma_start(stack[at * D:(at + count) * D, b % 2, 8 * n:8 * n + 8, :],
                                     src.rearrange("i d h n -> i d (h n)")).then_inc(stack_in[n][b % 2], 16)
                if (b, n) == (B - 1, 1):
                    sp.wait_ge(x_split, B)
                    sp.wait_ge(qk_rest, 4 * B)
                    sp.dma_start(ahead["w1_raw"][:, :, :], w1_d[0].rearrange("(k p) n -> p k n", p=P)).then_inc(ahead["w1_in"], 16)
                    sp.dma_start(ahead["w2_raw"][:, :, :], w2_d[0].rearrange("(k p) n -> p k n", p=P)).then_inc(ahead["w2_in"], 16)
            elif stage == "nm":
                sp.wait_ge(act_free, act_no[(stage, b, n)] + 1)
                for at in range(3):
                    sp.dma_start(qst[KQ + at:KQ + at + 1, b % 2, :, :], nmt[at * H:(at + 1) * H, :]).then_inc(rows_in, 16)
            elif stage == "picked":
                sp.wait_ge(best_ready, 1)
                sp.dma_start(chosen["left_f"][0:EARLY, :], best_f[:, P:P + 1]).then_inc(left_in, 16)
                sp.dma_start(chosen["left_gate"][0:EARLY, :], best[:, P:P + 1]).then_inc(left_in, 16)
            elif stage == "x1":
                sp.wait_ge(x1_ready, TT * (b + 1))
                for dst in (x1_d, acc_d):
                    sp.dma_start(dst[b * T:(b + 1) * T, :].rearrange("(t p) n -> p t n", p=P), res[:, b % 2, :, :]).then_inc(x1_out, 16)
        sp.wait_ge(x1_out, 32 * B)
        sp.wait_ge(left_in, 32)
        sp.wait_ge(ahead["w1_in"], 16)
        sp.wait_ge(ahead["w2_in"], 16)

    @block.gpsimd
    def _(pool):
        made = [0]

        def link(ins):
            made[0] += 1
            ins.then_inc(pool_step, 1)
            pool.wait_ge(pool_step, made[0])

        link(nc.gpsimd.memset(ident[:, :], 0.0))
        link(nc.gpsimd.affine_select(out=ident[:, :], in_=ident[:, :], compare_op=ALU.not_equal, fill=1.0, base=0,
                                     pattern=[[-1, P]], channel_multiplier=1))
        nc.gpsimd.tensor_copy(ident_b[:, :], ident[:, :]).then_inc(consts, 1)
        link(nc.gpsimd.memset(tri[:, :, :], 0.0))
        nc.gpsimd.affine_select(out=tri[:, :, :], in_=tri[:, :, :], compare_op=ALU.is_ge, fill=BIG_NEG, base=0,
                                pattern=[[0, 4], [-1, P]], channel_multiplier=1).then_inc(consts, 1)
        link(nc.gpsimd.memset(half[:, :], -0.5))
        nc.gpsimd.iota(base_i[:, :], pattern=[[T, EARLY]], base=0, channel_multiplier=0).then_inc(bases, 1)
        for stage, b, n in steps():
            if stage == "st":
                pool.wait_ge(exp_done, (b * PAIRS * UP) + n + 1)
                pair, u = n // UP, n % UP
                tiles = [c // P for _, _, c in ST_UNITS[u]]
                x = pt[:, (b * PAIRS + pair) % PT_RING, u, :].rearrange("p (j q) -> p j q", q=P)
                x = x[:, tiles[0]:tiles[-1] + 1:max(1, tiles[-1] - tiles[0]), :]
                nc.gpsimd.affine_select(out=x, in_=x, compare_op=ALU.is_ge, fill=0.0, base=0,
                                        pattern=[[0, len(tiles)], [1, P]], channel_multiplier=-1).then_inc(masked, 1)
            elif stage == "qk" and b:
                tile = 4 * b + n
                pool.wait_ge(qk_first, tile + 1)
                pool.wait_ge(act_free, act_no[(stage, b, n)] + 1)
                pool.wait_ge(qk_rest, tile)
                pool.wait_ge(parts_out[tile % 2], 48 * (tile // 2))
                link(nc.gpsimd.tensor_tensor(qk_r[:, :], qk_f[:, tile % 2, :], parts[:, tile % 2, 0, :], ALU.subtract))
                link(nc.gpsimd.tensor_tensor(parts[:, tile % 2, 1, :], qk_f[:, tile % 2, :], parts[:, tile % 2, 0, :], ALU.subtract))
                nc.gpsimd.tensor_tensor(parts[:, tile % 2, 2, :], qk_r[:, :], parts[:, tile % 2, 1, :], ALU.subtract).then_inc(qk_rest, 1)
            elif stage == "split":
                pool.wait_ge(x_hi, b + 1)
                nc.gpsimd.tensor_tensor(xt_lo[:, :, :], xt[:, :, :], xt_hi[:, :, :].bitcast(F32), ALU.subtract).then_inc(x_split, 1)
                if b == 0:
                    link(nc.gpsimd.memset(vaug[:, :, :, :, D:VW], 0.0))
                    nc.gpsimd.memset(vaug[:, :, :, :, D:D + 1], 1.0).then_inc(consts, 1)
                    pool.wait_ge(consts, 3)
                    two_ones = float(np.array([0x3F803F80], np.uint32).view(np.float32)[0])
                    nc.gpsimd.memset(kst[KQ:KM, :, :, :].rearrange("p a h n -> p (a h n)").bitcast(F32), two_ones).then_inc(consts, 1)
                    pool.wait_ge(consts, 4)
            elif stage == "x1":
                pool.wait_ge(var_ready, b + 1)
                nc.gpsimd.tensor_tensor(rstd[:, :], ve[:, :], half[:, :], ALU.pow).then_inc(rstd_ready, 1)
            elif stage == "fetch":
                pool.wait_ge(dve_free, dve_no[("picked", 0, 0)] + 1)
                pool.wait_ge(x1_out, 32 * EARLY)
                for q in range(2):
                    for at, j in enumerate(CHUNKS[q]):
                        nc.gpsimd.indirect_dma_start(ahead[f"tok{q}"][:, at, :], None, x1_d[0:EARLY * T, :],
                                                     bass.IndirectOffsetOnAxis(ap=chosen["tok_no"][:, j, 0:1], axis=0)).then_inc(ahead[f"tok_in{q}"], 16)

    @block.scalar
    def _(act):
        for stage, b, n in steps():
            if stage in BY_ACT:
                act.wait_ge(act_ready, act_no[(stage, b, n)] + 1)
            if stage == "st":
                at, slot = b * PAIRS * UP + n, b * PAIRS + n // UP
                act.wait_ge(st_done, at + 1)
                if n % UP == 0 and slot >= PT_RING:
                    act.wait_ge(av_done, (slot - PT_RING) // 2 + 1)
                nc.scalar.activation(pt[:, slot % PT_RING, n % UP, :], st_ps[at % ST_RING][:, :], ACT.Exp,
                                     scale=S_SCALE).then_inc(exp_done, 1)
            elif stage == "split":
                act.wait_ge(xt_in, 16 * (b + 1))
                if b >= 1:
                    act.wait_ge(act_ready, act_no[("v", b - 1, 1)] + 1)
                    act.wait_ge(x_split, b)
                nc.scalar.activation(xt_hi[:, :, :], xt[:, :, :], ACT.Copy).then_inc(x_hi, 1)
            elif stage == "av" and n == 3:
                act.wait_ge(av_done, b + 1)
                if b >= 2:
                    last = ("onorm", (b - 2) // GROUPS, (b - 2) % GROUPS)
                    act.wait_ge(dve_ready, dve_no[last] + 1)
                nc.scalar.activation(av_sb[:, b % 2, :], av_ps[:, :], ACT.Copy).then_inc(av_out, 1)
            elif stage == "qk":
                tile = 4 * b + n
                if tile >= 2:
                    act.wait_ge(qk_rest, tile - 1)
                    act.wait_ge(parts_out[tile % 2], 48 * (tile // 2))
                bank = act_bank(stage, b, n)
                nc.scalar.activation(parts[:, tile % 2, 0, :], bank[:, :], ACT.Copy).then_inc(qk_first, 1)
                nc.scalar.activation(qk_f[:, tile % 2, :], bank[:, :], ACT.Copy).then_inc(act_free, 1)
            elif stage == "v":
                if b == 0 and n == 0:
                    act.wait_ge(consts, 3)
                if b >= 3:
                    act.wait_ge(av_done, (b - 2) * GROUPS)
                src = act_bank(stage, b, n)[:, :].rearrange("p (t h d) -> p t h d", t=2, h=H)
                for t in range(2):
                    ins = nc.scalar.activation(vaug[:, b % 3, 2 * n + t, :, 0:D], src[:, t, :, :], ACT.Copy)
                ins.then_inc(act_free, 1)
            elif stage == "nm":
                if b >= 1:
                    act.wait_ge(rows_in, 48 * b)
                nc.scalar.activation(nmt[:, :], nm_ps[0:3 * H, 0:T], ACT.Copy).then_inc(act_free, 1)
            elif stage == "ot":
                if b >= 1:
                    act.wait_ge(dve_ready, dve_no[("proj", b - 1, 1)] + 1)
                nc.scalar.activation(o_t[:, n, :], act_ps[:, :], ACT.Copy).then_inc(act_free, 1)
            elif stage == "x1t":
                if b >= 1:
                    act.wait_ge(dve_ready, dve_no[("logit", b - 1, 0)] + 1)
                nc.scalar.activation(x1t[:, n, :], act_ps[:, :], ACT.Copy).then_inc(act_free, 1)
            elif stage == "logit":
                act.wait_ge(dve_free, dve_no[(stage, b, n)] + 1)
                if b >= 1:
                    act.wait_ge(scored, b)
                nc.scalar.activation(lge[:, :, :], lg[:, :, :], ACT.Exp).then_inc(lexp, 1)

    @block.vector
    def _(dve):
        made = [0]

        def link(ins):
            made[0] += 1
            ins.then_inc(dve_step, 1)
            dve.wait_ge(dve_step, made[0])

        dve.wait_ge(w_in, 16)
        raw = pt[:, 0, 0:3, :].rearrange("p a n -> p (a n)").rearrange("p (k n) -> p k n", k=KC)
        link(nc.vector.tensor_copy(w_hi[:, :, :], raw))
        nc.vector.tensor_tensor(w_lo[:, :, :], raw, w_hi[:, :, :].bitcast(F32), ALU.subtract).then_inc(w_split, 1)
        for stage, b, n in steps():
            if stage in BY_DVE:
                dve.wait_ge(dve_ready, dve_no[(stage, b, n)] + 1)
            if stage == "nat":
                qb, h0, heads = N_UNITS[n]
                at = b * NU + n
                dve.wait_ge(nat_done, at + 1)
                src = n_ps[at % N_RING][:, 0:heads * (qb + 1) * P].rearrange("p (h k) -> p h k", h=heads)
                nc.vector.tensor_reduce(out=nmax[:, b % 2, qb, h0:h0 + heads], in_=src, axis=AX.X, op=ALU.max, negate=True).then_inc(max_done, 1)
            elif stage == "qk" and b == 0:
                dve.wait_ge(qk_first, n + 1)
                dve.wait_ge(act_free, act_no[(stage, b, n)] + 1)
                if n:
                    dve.wait_ge(qk_rest, n)
                if n >= 2:
                    dve.wait_ge(parts_out[n % 2], 48 * (n // 2))
                link(nc.vector.tensor_tensor(qk_r[:, :], qk_f[:, n % 2, :], parts[:, n % 2, 0, :], ALU.subtract))
                link(nc.vector.tensor_tensor(parts[:, n % 2, 1, :], qk_f[:, n % 2, :], parts[:, n % 2, 0, :], ALU.subtract))
                nc.vector.tensor_tensor(parts[:, n % 2, 2, :], qk_r[:, :], parts[:, n % 2, 1, :], ALU.subtract).then_inc(qk_rest, 1)
            elif stage == "nmcut":
                dve.wait_ge(max_done, NU * (b + 1))
                if b >= 1:
                    dve.wait_ge(act_ready, act_no[("nm", b - 1, 0)] + 1)
                link(nc.vector.tensor_copy(nm3[:, :, 0, :], nmax[:, b % 2, :, :]))
                link(nc.vector.tensor_tensor(nmax_r[:, :, :], nmax[:, b % 2, :, :], nm3[:, :, 0, :], ALU.subtract))
                link(nc.vector.tensor_copy(nm3[:, :, 1, :], nmax_r[:, :, :]))
                nc.vector.tensor_tensor(nm3[:, :, 2, :], nmax_r[:, :, :], nm3[:, :, 1, :], ALU.subtract).then_inc(nm_parts, 1)
            elif stage == "onorm":
                src = dve_ps[:, :].rearrange("p (t j v) -> p t j v", t=TT, j=4)
                link(nc.vector.reciprocal(rden[:, :, :], src[:, :, :, D]))
                if b >= 1 and n == 0:
                    dve.wait_ge(act_ready, act_no[("ot", b - 1, 1)] + 1)
                dst = o_nat[:, :, 4 * D * n:4 * D * (n + 1)].rearrange("p t (j d) -> p t j d", j=4)
                nc.vector.tensor_tensor(dst, src[:, :, :, 0:D], rden[:, :, :].unsqueeze(3).to_broadcast([P, TT, 4, D]), ALU.mult).then_inc(dve_free, 1)
            elif stage == "proj":
                if n == 0:
                    dve.wait_ge(res_in[b % 2], 16 * (b // 2 + 1))
                rows = res[:, b % 2, 2 * n:2 * n + 2, :].rearrange("p t c -> p (t c)")
                nc.vector.scalar_tensor_tensor(out=rows, in0=dve_ps[:, :], scalar=O_SCALE, in1=rows,
                                               op0=ALU.mult, op1=ALU.add).then_inc(dve_free, 1)
                dve.wait_ge(dve_free, dve_no[(stage, b, n)] + 1)
                for t in (2 * n, 2 * n + 1):
                    ins = nc.vector.bn_stats(stats[:, t, :], res[:, b % 2, t, :])
                    if t % 2 == 0:
                        ins.then_inc(dve_step, 1)
                        made[0] += 1
                link(ins)
                for t in (2 * n, 2 * n + 1):
                    ins = nc.vector.bn_aggr(mv[:, t, :], stats[:, t, :])
                    if t % 2 == 0:
                        ins.then_inc(dve_step, 1)
                        made[0] += 1
                link(ins)
                if n == 1:
                    nc.vector.tensor_scalar_add(ve[:, :], mv[:, :, 1], EPS).then_inc(var_ready, 1)
            elif stage == "x1":
                dve.wait_ge(rstd_ready, b + 1)
                for t in range(TT):
                    row = res[:, b % 2, t, :]
                    nc.vector.tensor_scalar(row, row, mv[:, t, 0:1], rstd[:, t:t + 1], ALU.subtract, ALU.mult).then_inc(x1_ready, 1)
            elif stage == "logit":
                src = dve_ps[:, 0:TT * E].rearrange("p (t e) -> p t e", t=TT)
                link(nc.vector.tensor_reduce(out=lmax[:, :], in_=src, axis=AX.X, op=ALU.max))
                if b >= 1:
                    dve.wait_ge(lexp, b)
                nc.vector.tensor_tensor(lg[:, :, :], src, lmax[:, :].unsqueeze(2).to_broadcast([P, TT, E]), ALU.subtract).then_inc(dve_free, 1)
            elif stage == "pick":
                nc.vector.tensor_copy(row_pool[0][:, :], dve_ps[0:early, :]).then_inc(dve_free, 1)
                dve.wait_ge(dve_free, dve_no[(stage, b, n)] + 1)
            elif stage == "round":
                pick_round(nc, link, row_pool, best, best_at, n)
                if n == ROUNDS - 1:
                    nc.vector.tensor_copy(best_f[:, :], best_at[:, :]).then_inc(best_ready, 1)
            elif stage == "picked":
                dve.wait_ge(bases, 1)
                src = dve_ps[:, 0:2 * early].rearrange("p (a b e) -> p a b e", a=2, b=EARLY)
                link(nc.vector.tensor_tensor(chosen["tok_no"][:, 0:EARLY, :], src[:, 0, :, :],
                                             base_i[:, :].unsqueeze(2).to_broadcast([P, EARLY, E]), ALU.add))
                nc.vector.tensor_copy(chosen["gate"][:, 0:EARLY, :], src[:, 1, :, :]).then_inc(dve_free, 1)
            elif stage == "score":
                dve.wait_ge(lexp, b + 1)
                link(nc.vector.tensor_reduce(out=lsum[:, :], in_=lge[:, :, :], axis=AX.X, op=ALU.add))
                link(nc.vector.reciprocal(linv[:, :], lsum[:, :]))
                nc.vector.tensor_tensor(scores[:, :, b, :], lge[:, :, :], linv[:, :].unsqueeze(2).to_broadcast([P, TT, E]), ALU.mult).then_inc(scored, 1)

    @block.tensor
    def _(pe):
        pe.wait_ge(w_split, 1)
        for stage, b, n in steps():
            if stage in BY_ACT and act_no[(stage, b, n)] >= act_banks(stage, b):
                pe.wait_ge(act_free, act_no[(stage, b, n)] - act_banks(stage, b) + 1)
            if stage in BY_DVE and dve_no[(stage, b, n)]:
                pe.wait_ge(dve_free, dve_no[(stage, b, n)])
            if stage == "st":
                at = b * PAIRS * UP + n
                pair, u = n // UP, n % UP
                if b == 0 and n == 0:
                    pe.wait_ge(consts, 4)
                if n == 0:
                    pe.wait_ge(rows_in, 48 * (b + 1))
                if at >= ST_RING:
                    pe.wait_ge(exp_done, at - ST_RING + 1)
                for hh, kb, c in ST_UNITS[u]:
                    h = 2 * pair + hh
                    ins = nc.tensor.matmul(st_ps[at % ST_RING][:, c:c + T - kb * P], kst[0:KM, b % 2, h, kb * P:(kb + 1) * P],
                                           qst[0:KM, b % 2, h, kb * P:T], start=True, stop=True)
                ins.then_inc(st_done, 1)
            elif stage == "nat":
                qb, h0, heads = N_UNITS[n]
                at = b * NU + n
                if b == 0 and n == 0:
                    pe.wait_ge(consts, 2)
                if n % (NU // 2) == 0:
                    pe.wait_ge(stack_in[n // (NU // 2)][b % 2], 16 * (len(K_RUNS) + len(Q_RUNS)) * (b // 2 + 1))
                if at >= N_RING:
                    pe.wait_ge(max_done, at - N_RING + 1)
                bank, w = n_ps[at % N_RING], (qb + 1) * P
                if qb == 0:
                    nc.tensor.matmul(bank[:, :], ident_b[:, :], tri[:, :, :].rearrange("p a k -> p (a k)"), start=True, stop=False)
                for j in range(heads):
                    h = h0 + j
                    ins = nc.tensor.matmul(bank[:, j * w:(j + 1) * w], qst[0:KQ, b % 2, h, qb * P:(qb + 1) * P],
                                           kst[0:KQ, b % 2, h, 0:w], start=qb > 0, stop=qb > 0 or j == heads - 1)
                    if qb > 0:
                        ins = nc.tensor.matmul(bank[:, (j + 1) * w - P:(j + 1) * w], ident_b[:, :], tri[:, 0, :], start=False, stop=True,
                                               skip_group_check=True)
                ins.then_inc(nat_done, 1)
            elif stage == "av":
                seq, group = b // GROUPS, b % GROUPS
                if n == 0:
                    pe.wait_ge(masked, (2 * b + 2) * UP)
                    if b:
                        pe.wait_ge(av_out, b)
                    if group == 0:
                        pe.wait_ge(act_free, act_no[("v", seq, 1)] + 1)
                for j in range(4):
                    h = 4 * group + j
                    u, c = ST_AT[(h % 2, n)]
                    ins = nc.tensor.matmul(av_ps[VW * j:VW * (j + 1), n * P:T], vaug[:, seq % 3, n, h, :],
                                           pt[:, (seq * PAIRS + h // 2) % PT_RING, u, c:c + T - n * P], start=n == 0, stop=n == TT - 1,
                                           skip_group_check=True)
                if n == TT - 1:
                    ins.then_inc(av_done, 1)
            elif stage == "onorm":
                group = b * GROUPS + n
                pe.wait_ge(av_out, group + 1)
                for t in range(TT):
                    ins = nc.tensor.transpose(dve_ps[:, t * P:(t + 1) * P], av_sb[:, group % 2, t * P:(t + 1) * P], ident[:, :])
                ins.then_inc(dve_ready, 1)
            elif stage == "qk":
                which, half_ = n % 2, n // 2
                pe.wait_ge(x_split, b + 1)
                cols = slice(which * C + half_ * P, which * C + half_ * P + P)
                for at, (w, x) in enumerate(((w_hi, xt_hi), (w_hi, xt_lo), (w_lo, xt_hi))):
                    for k in range(KC):
                        ins = nc.tensor.matmul(act_bank(stage, b, n)[:, :], w[:, k, cols], x[:, k, :], start=at + k == 0, stop=at == 2 and k == KC - 1)
                ins.then_inc(act_ready, 1)
            elif stage == "v":
                for t in range(2):
                    toks = slice((2 * n + t) * P, (2 * n + t + 1) * P)
                    for at, (w, x) in enumerate(((w_hi, xt_hi), (w_hi, xt_lo), (w_lo, xt_hi))):
                        for k in range(KC):
                            ins = nc.tensor.matmul(act_bank(stage, b, n)[:, t * C:(t + 1) * C], x[:, k, toks], w[:, k, 2 * C:3 * C],
                                                   start=at + k == 0, stop=at == 2 and k == KC - 1)
                ins.then_inc(act_ready, 1)
            elif stage == "nm":
                pe.wait_ge(nm_parts, b + 1)
                for t in range(TT):
                    ins = nc.tensor.transpose(nm_ps[0:3 * H, t * P:(t + 1) * P], nm3[:, t, :, :].rearrange("p i h -> p (i h)"), ident_b[:, :])
                ins.then_inc(act_ready, 1)
            elif stage == "ot":
                pe.wait_ge(dve_free, dve_no[("onorm", b, 3)] + 1)
                for t in range(TT):
                    ins = nc.tensor.transpose(act_ps[:, t * P:(t + 1) * P], o_nat[:, t, n * P:(n + 1) * P], ident[:, :])
                ins.then_inc(act_ready, 1)
            elif stage == "proj":
                if b == 0 and n == 0:
                    pe.wait_ge(wp_in, 32)
                pe.wait_ge(act_free, act_no[("ot", b, 1)] + 1)
                for t in range(2):
                    toks = slice((2 * n + t) * P, (2 * n + t + 1) * P)
                    for k in range(KC):
                        ins = nc.tensor.matmul(dve_ps[:, t * C:(t + 1) * C], o_t[:, k, toks], wp[:, k, :], start=k == 0, stop=k == KC - 1)
                ins.then_inc(dve_ready, 1)
            elif stage == "x1t":
                pe.wait_ge(x1_ready, TT * (b + 1))
                for t in range(TT):
                    ins = nc.tensor.transpose(act_ps[:, t * P:(t + 1) * P], res[:, b % 2, t, n * P:(n + 1) * P], ident[:, :])
                ins.then_inc(act_ready, 1)
            elif stage == "pick":
                pe.wait_ge(scored, EARLY)
                for t in range(TT):
                    ins = nc.tensor.transpose(dve_ps[0:early, t * P:(t + 1) * P],
                                              scores[:, t, 0:EARLY, :].rearrange("p b e -> p (b e)"), ident[:, :])
                ins.then_inc(dve_ready, 1)
            elif stage == "picked":
                pe.wait_ge(best_ready, 1)
                nc.tensor.transpose(dve_ps[:, 0:early], best_f[:, 0:P], ident[0:early, 0:early])
                nc.tensor.transpose(dve_ps[:, early:2 * early], best[:, 0:P], ident[0:early, 0:early]).then_inc(dve_ready, 1)
            elif stage == "logit":
                pe.wait_ge(act_free, act_no[("x1t", b, 1)] + 1)
                for t in range(TT):
                    for k in range(KC):
                        ins = nc.tensor.matmul(dve_ps[:, t * E:(t + 1) * E], x1t[:, k, t * P:(t + 1) * P], rw[:, k, :],
                                               start=k == 0, stop=k == KC - 1)
                ins.then_inc(dve_ready, 1)


LEFT = B
CHUNKS = ((0, 1, 2), (3, 4, 5), (6, 7, LEFT))
NC = len(CHUNKS)
LATE = B - EARLY
JOBS = [(0, 0), (0, 1), (1, 0), (1, 1), (0, 2), (1, 2)] + [(e, c) for e in range(2, E - 1) for c in range(NC)]
JOBS += [(E - 1, c) for c in (2, 0, 1)]
NQ = len(JOBS)
H_RING, Y_RING, TOK_RING, G_RING = 3, 2, 3, 3
TURN_AT, FETCH_AT = 6, 7
PICKED_AT = (2, 1)
ROUNDS_IN = (5, 6, 6)
DOWN_AT = (2, 5, 8)


def rows_of(tile):
    return B if tile == LEFT else P


def job(q):
    e, c = JOBS[q]
    return e, CHUNKS[c], sum(rows_of(j) for j in CHUNKS[c])


FIRST_JOB = {e: min(q for q in range(NQ) if JOBS[q][0] == e) for e in range(E)}
LAST_JOB = {e: max(q for q in range(NQ) if JOBS[q][0] == e) for e in range(E)}


FINISH = [((NQ - 2, 0), "load", 6), ((NQ - 2, 1), "load", 7), ((NQ - 2, 4), "norm", 6), ((NQ - 2, 7), "norm", 7),
          ((NQ - 1, 0), "load", 0), ((NQ - 1, 1), "load", 1), ((NQ - 1, 3), "load", 2), ((NQ - 1, 4), "norm", 0),
          ((NQ - 1, 5), "load", 3), ((NQ - 1, 8), "load", 4), ((NQ - 1, 9), "load", 5)]
FINISH += [((NQ - 1, 9), "norm", b) for b in range(1, 6)]
FIN_NO = {b: n for n, b in enumerate(b for _, stage, b in FINISH if stage == "load")}
FIN_RING = 4


def cut_at(stage, e):
    if stage == "cut1":
        return FIRST_JOB[e] - 2, 1
    return max(FIRST_JOB[e] - 2, LAST_JOB[e - 2] + 1 if e >= 2 else 0), 4


def expert_steps():
    rounds = 0
    yield "cut1", 0, 0
    yield "turn", 0, 0
    yield "cut2", 0, 0
    yield "rows", 0, 0
    for q in range(-1, NQ):
        for m in range(KH + 2):
            if q + 1 < NQ and m < KH:
                yield "up", q + 1, m
            for e in range(1, E):
                for stage in ("cut1", "cut2"):
                    if (q, m) == cut_at(stage, e):
                        yield stage, e, 0
            if q + 1 < len(ROUNDS_IN) and (m + 1) * ROUNDS_IN[q + 1] // (KH + 1) > m * ROUNDS_IN[q + 1] // (KH + 1):
                yield "round", 0, rounds
                rounds += 1
            for at, stage, b in FINISH:
                if (q, m) == at:
                    yield stage, b, 0
            if (q, m) == PICKED_AT:
                yield "picked", 0, 0
            if m == (1 if q < 0 else TURN_AT) and q + 2 < NQ:
                yield "turn", q + 2, 0
            if m == FETCH_AT and TOK_RING <= q + 3 < NQ:
                yield "fetch", q + 3, 0
            if q >= 0 and m in DOWN_AT:
                yield "down", q, m // 3


def adds_before():
    count, out = [0] * (B + 1), {}
    for q, (e, c) in enumerate(JOBS):
        for j in CHUNKS[c]:
            others = [x for x in (range(B + 1) if j == LEFT else (j, LEFT))]
            out[q, j] = {x: sum(1 for qq in range(q) if x in CHUNKS[JOBS[qq][1]] and JOBS[qq][0] != e) for x in others}
            for x in others:
                if x != j:
                    out[q, j][x] = max([n + 1 for n, qq in enumerate([qq for qq in range(q) if x in CHUNKS[JOBS[qq][1]]])
                                        if JOBS[qq][0] != e], default=0)
            count[j] += 1
    return out


ADDS = adds_before()


def experts(nc, ctx, x1_d, acc_d, w1_d, b1_d, w2_d, b2_d, out_d, ident, scores, chosen, ahead):
    def sb(name, shape, dt):
        return ctx.enter_context(nc.sbuf_tensor(name, shape, dt))

    def sem(name):
        return ctx.enter_context(nc.semaphore(name))

    late = LATE * E
    tok_no, gate, left_f, left_gate = (chosen[n] for n in ("tok_no", "gate", "left_f", "left_gate"))
    row_pool = [sb(f"late_pool{n}", [late, T], F32) for n in range(2)]
    best = sb("late_best", [late, 8 * ROUNDS], F32)
    best_at = sb("late_best_at", [late, 8 * ROUNDS], U32)
    best_f = sb("late_best_f", [late, 8 * ROUNDS], F32)
    base_i = sb("late_base_i", [P, LATE, E], I32)
    lbase_i = sb("lbase_i", [B, E], I32)
    left_no = sb("left_no", [B, E], U32)
    b1 = sb("b1", [P, E, KH], F32)
    b2 = sb("b2", [P, E, C], F32)
    w1_raw, w2_raw = ahead["w1_raw"], ahead["w2_raw"]
    w1_hi = sb("w1_hi", [P, 2, KC, HID], F32R)
    w1_lo = sb("w1_lo", [P, 2, KC, HID], F32R)
    w2_hi = sb("w2_hi", [P, 2, KH, C], F32R)
    w2_lo = sb("w2_lo", [P, 2, KH, C], F32R)
    tok = [ahead["tok0"], ahead["tok1"]] + [sb(f"tok{n}", [P, 3, C], F32) for n in range(2, TOK_RING)]
    tt_hi = sb("tt_hi", [P, TOK_RING, KC, 3 * P], F32R)
    tt_lo = sb("tt_lo", [P, TOK_RING, KC, 3 * P], F32R)
    g = sb("g", [P, G_RING, 3 * P], F32)
    h_hi = sb("h_hi", [P, 2, KH, 3 * P], F32R)
    h_lo = sb("h_lo", [P, 2, KH, 3 * P], F32R)
    y = sb("y", [P, B + 1, C], F32)
    fin = sb("fin", [P, FIN_RING, TT, C], F32)
    stats2 = sb("stats2", [P, TT, 6], F32)
    mv2 = sb("mv2", [P, FIN_RING, TT, 2], F32)
    ve2 = sb("ve2", [P, FIN_RING, TT], F32)
    nmean = sb("nmean", [P, FIN_RING, TT], F32)
    half2 = sb("half2", [P, TT], F32)
    rstd2 = sb("rstd2", [P, FIN_RING, TT], F32)
    shift2 = sb("shift2", [P, FIN_RING, TT], F32)

    h_ps = [ctx.enter_context(nc.psum_tensor(f"h_ps{n}", [P, T], F32)) for n in range(H_RING)]
    y_ps = [ctx.enter_context(nc.psum_tensor(f"y_ps{n}", [P, T], F32)) for n in range(Y_RING)]
    tp_ps = [ctx.enter_context(nc.psum_tensor(f"tp_ps{n}", [P, T], F32)) for n in range(KC)]
    pick_ps = ctx.enter_context(nc.psum_tensor("pick_ps", [P, T], F32))

    rows_ready = sem("rows_ready")
    rows_taken = sem("rows_taken")
    dve_step2 = sem("dve_step2")
    bases = sem("bases2")
    best_ready = sem("best_ready2")
    best_t = sem("best_t")
    left_in = sem("left_in2")
    picked = sem("picked")
    bias_in = sem("bias_in")
    w1_in, w2_in = ahead["w1_in"], ahead["w2_in"]
    w1_top, w2_top = sem("w1_top"), sem("w2_top")
    w1_cut, w2_cut = sem("w1_cut"), sem("w2_cut")
    tok_in = [ahead["tok_in0"], ahead["tok_in1"]] + [sem(f"tok_in{n}") for n in range(2, TOK_RING)]
    tp_done = sem("tp_done")
    tp_hi = sem("tp_hi")
    tp_lo = sem("tp_lo")
    h_done = sem("h_done")
    g_done = sem("g_done")
    g_hi, g_lo = sem("g_hi"), sem("g_lo")
    y_done = sem("y_done")
    y_out = sem("y_out")
    y_ready = sem("y_ready")
    added = [sem(f"added{n}") for n in range(B + 1)]
    fin_in = [sem(f"fin_in{n}") for n in range(FIN_RING)]
    fin_step = sem("fin_step")
    fin_var, fin_rstd, fin_done = sem("fin_var"), sem("fin_rstd"), sem("fin_done")
    fin_out = [sem(f"fin_out{n}") for n in range(FIN_RING)]

    block = ctx.enter_context(nc.Block())

    @block.sync
    def _(sp):
        def load_w1(e):
            sp.wait_ge(w1_cut, e)
            sp.dma_start(w1_raw[:, :, :], w1_d[e].rearrange("(k p) n -> p k n", p=P)).then_inc(w1_in, 16)

        def load_w2(e):
            sp.wait_ge(w2_cut, e)
            sp.dma_start(w2_raw[:, :, :], w2_d[e].rearrange("(k p) n -> p k n", p=P)).then_inc(w2_in, 16)

        sp.dma_start(b1[:, :, :], b1_d.rearrange("p (e m) -> p e m", e=E)).then_inc(bias_in, 16)
        sp.dma_start(b2[:, :, :], b2_d.rearrange("e c -> (e c)").rearrange("(o n) -> o n", o=1).to_broadcast([P, E * C])).then_inc(bias_in, 16)
        for stage, q, n in expert_steps():
            if stage == "cut1" and q + 1 < E:
                load_w1(q + 1)
            elif stage == "cut2" and q + 1 < E:
                load_w2(q + 1)
            elif stage == "load":
                at = FIN_NO[q]
                sp.wait_ge(added[q], 16 * E)
                sp.wait_ge(added[LEFT], 16 * E)
                if at >= FIN_RING:
                    sp.wait_ge(fin_out[at % FIN_RING], 16 * (at // FIN_RING))
                sp.dma_start(fin[:, at % FIN_RING, :, :], acc_d[q * T:(q + 1) * T, :].rearrange("(t p) n -> p t n", p=P)).then_inc(fin_in[at % FIN_RING], 16)
            elif stage == "picked":
                sp.wait_ge(best_ready, 1)
                sp.dma_start(left_f[EARLY:B, :], best_f[:, P:P + 1]).then_inc(left_in, 16)
                sp.dma_start(left_gate[EARLY:B, :], best[:, P:P + 1]).then_inc(left_in, 16)
        for n in range(FIN_RING):
            sp.wait_ge(fin_out[n], 16 * B // FIN_RING)

    @block.gpsimd
    def _(pool):
        def choice(e, j):
            return left_no[:, e:e + 1] if j == LEFT else tok_no[:, j, e:e + 1]

        def gather(q):
            e, tiles, _ = job(q)
            if q >= TOK_RING:
                pool.wait_ge(tp_done, KC * (q - TOK_RING + 1))
            if LEFT in tiles:
                pool.wait_ge(picked, 2)
            for at, j in enumerate(tiles):
                nc.gpsimd.indirect_dma_start(tok[q % TOK_RING][0:rows_of(j), at, :], None, x1_d[:, :],
                                             bass.IndirectOffsetOnAxis(ap=choice(e, j), axis=0)).then_inc(tok_in[q % TOK_RING], 16)

        nc.gpsimd.iota(base_i[:, :, :], pattern=[[T, LATE], [0, E]], base=EARLY * T, channel_multiplier=0).then_inc(bases, 1)
        nc.gpsimd.iota(lbase_i[:, :], pattern=[[0, E]], base=0, channel_multiplier=T).then_inc(bases, 1)
        nc.gpsimd.memset(half2[:, :], -0.5).then_inc(bases, 1)
        gather(2)
        for stage, q, n in expert_steps():
            if stage == "fetch":
                gather(q)
            elif stage in ("cut1", "cut2") and q:
                raw, hi, lo, top, done = ((w1_raw, w1_hi, w1_lo, w1_top, w1_cut) if stage == "cut1" else
                                          (w2_raw, w2_hi, w2_lo, w2_top, w2_cut))
                pool.wait_ge(top, q + 1)
                nc.gpsimd.tensor_tensor(lo[:, q % 2, :, :], raw[:, :, :], hi[:, q % 2, :, :].bitcast(F32), ALU.subtract).then_inc(done, 1)
            elif stage == "down":
                e, tiles, _ = job(q)
                j = tiles[n]
                pool.wait_ge(y_ready, 3 * q + n + 1)
                for other, count in ADDS[q, j].items():
                    if count:
                        pool.wait_ge(added[other], 16 * count)
                nc.gpsimd.indirect_dma_start(acc_d[:, :], bass.IndirectOffsetOnAxis(ap=choice(e, j), axis=0),
                                             y[0:rows_of(j), j, :], None, compute_op=ALU.add).then_inc(added[j], 16)
            elif stage == "norm":
                at = FIN_NO[q]
                pool.wait_ge(bases, 3)
                pool.wait_ge(fin_var, 2 * (at + 1))
                if at >= FIN_RING:
                    pool.wait_ge(fin_done, TT * (at - FIN_RING + 1))
                nc.gpsimd.tensor_tensor(rstd2[:, at % FIN_RING, :], ve2[:, at % FIN_RING, :], half2[:, :], ALU.pow).then_inc(fin_rstd, 1)
                pool.wait_ge(fin_rstd, 2 * at + 1)
                nc.gpsimd.tensor_tensor(shift2[:, at % FIN_RING, :], nmean[:, at % FIN_RING, :], rstd2[:, at % FIN_RING, :], ALU.mult).then_inc(fin_rstd, 1)

    @block.scalar
    def _(act):
        for stage, q, n in expert_steps():
            if stage == "turn":
                _, _, cols = job(q)
                for k in range(KC):
                    act.wait_ge(tp_done, KC * q + k + 1)
                    if q >= TOK_RING:
                        act.wait_ge(h_done, KH * (q - TOK_RING + 1))
                    nc.scalar.activation(tt_hi[:, q % TOK_RING, k, 0:cols], tp_ps[k][:, 0:cols], ACT.Copy).then_inc(tp_hi, 1)
            elif stage == "up":
                e, _, cols = job(q)
                at = KH * q + n
                if at == 0:
                    act.wait_ge(bias_in, 32)
                act.wait_ge(h_done, at + 1)
                if at >= G_RING:
                    act.wait_ge(g_lo, at - G_RING + 1)
                nc.scalar.activation(g[:, at % G_RING, 0:cols], h_ps[at % H_RING][:, 0:cols], ACT.Gelu,
                                     bias=b1[:, e, n:n + 1]).then_inc(g_done, 1)
                if q >= 2 and n == 0:
                    act.wait_ge(y_done, 3 * (q - 1))
                act.wait_ge(g_done, at + 1)
                nc.scalar.activation(h_hi[:, q % 2, n, 0:cols], g[:, at % G_RING, 0:cols], ACT.Copy).then_inc(g_hi, 1)
            elif stage in ("cut1", "cut2"):
                raw, hi, came, done = (w1_raw, w1_hi, w1_in, w1_top) if stage == "cut1" else (w2_raw, w2_hi, w2_in, w2_top)
                if q >= 2 and stage == "cut1":
                    act.wait_ge(h_done, KH * (LAST_JOB[q - 2] + 1))
                elif q >= 2:
                    act.wait_ge(y_done, 3 * (LAST_JOB[q - 2] + 1))
                act.wait_ge(came, 16 * (q + 1))
                nc.scalar.activation(hi[:, q % 2, :, :], raw[:, :, :], ACT.Copy).then_inc(done, 1)
        for b, at in FIN_NO.items():
            act.wait_ge(fin_rstd, 2 * (at + 1))
            for t in range(TT):
                row = fin[:, at % FIN_RING, t, :]
                nc.scalar.activation(row, row, ACT.Identity, bias=shift2[:, at % FIN_RING, t:t + 1],
                                     scale=rstd2[:, at % FIN_RING, t:t + 1]).then_inc(fin_done, 1)
            act.wait_ge(fin_done, TT * (at + 1))
            act.dma_start(out_d[b * T:(b + 1) * T, :].rearrange("(t p) n -> p t n", p=P), fin[:, at % FIN_RING, :, :]).then_inc(fin_out[at % FIN_RING], 16)

    @block.vector
    def _(dve):
        made = [0]

        def link(ins):
            made[0] += 1
            ins.then_inc(dve_step2, 1)
            dve.wait_ge(dve_step2, made[0])

        for stage, q, n in expert_steps():
            if stage == "turn":
                _, _, cols = job(q)
                for k in range(KC):
                    dve.wait_ge(tp_hi, KC * q + k + 1)
                    nc.vector.tensor_tensor(tt_lo[:, q % TOK_RING, k, 0:cols], tp_ps[k][:, 0:cols],
                                            tt_hi[:, q % TOK_RING, k, 0:cols].bitcast(F32), ALU.subtract).then_inc(tp_lo, 1)
            elif stage == "round":
                if n == 0:
                    dve.wait_ge(rows_ready, 1)
                    nc.vector.tensor_copy(row_pool[0][:, :], pick_ps[0:late, :]).then_inc(rows_taken, 1)
                    dve.wait_ge(rows_taken, 1)
                pick_round(nc, link, row_pool, best, best_at, n)
                if n == ROUNDS - 1:
                    nc.vector.tensor_copy(best_f[:, :], best_at[:, :]).then_inc(best_ready, 1)
            elif stage == "picked":
                dve.wait_ge(best_t, 1)
                dve.wait_ge(bases, 3)
                src = pick_ps[:, 0:2 * late].rearrange("p (a b e) -> p a b e", a=2, b=LATE)
                link(nc.vector.tensor_copy(gate[:, EARLY:B, :], src[:, 1, :, :]))
                nc.vector.tensor_tensor(tok_no[:, EARLY:B, :], src[:, 0, :, :], base_i[:, :, :], ALU.add).then_inc(picked, 1)
                dve.wait_ge(left_in, 32)
                nc.vector.tensor_tensor(left_no[:, :], left_f[:, :], lbase_i[:, :], ALU.add).then_inc(picked, 1)
            elif stage == "up":
                _, _, cols = job(q)
                at = KH * q + n
                if q >= 2 and n == 0:
                    dve.wait_ge(y_done, 3 * (q - 1))
                dve.wait_ge(g_hi, at + 1)
                nc.vector.tensor_tensor(h_lo[:, q % 2, n, 0:cols], g[:, at % G_RING, 0:cols],
                                        h_hi[:, q % 2, n, 0:cols].bitcast(F32), ALU.subtract).then_inc(g_lo, 1)
            elif stage == "down":
                e, tiles, _ = job(q)
                j, at = tiles[n], 3 * q + n
                rows, before = rows_of(j), sum(j in CHUNKS[c] for _, c in JOBS[:q])
                dve.wait_ge(y_done, at + 1)
                if at == 0:
                    dve.wait_ge(bias_in, 32)
                if before:
                    dve.wait_ge(added[j], 16 * before)
                nc.vector.tensor_tensor(y[0:rows, j, :], y_ps[at % Y_RING][0:rows, 0:C], b2[0:rows, e, :], ALU.add).then_inc(y_out, 1)
                dve.wait_ge(y_out, at + 1)
                by = left_gate[:, e:e + 1] if j == LEFT else gate[:, j, e:e + 1]
                nc.vector.tensor_scalar(y[0:rows, j, :], y[0:rows, j, :], by, None, ALU.mult).then_inc(y_ready, 1)
            elif stage in ("cut1", "cut2") and q == 0:
                raw, hi, lo, top, done = ((w1_raw, w1_hi, w1_lo, w1_top, w1_cut) if stage == "cut1" else
                                          (w2_raw, w2_hi, w2_lo, w2_top, w2_cut))
                dve.wait_ge(top, 1)
                nc.vector.tensor_tensor(lo[:, 0, :, :], raw[:, :, :], hi[:, 0, :, :].bitcast(F32), ALU.subtract).then_inc(done, 1)
            elif stage == "norm":
                at = FIN_NO[q]
                dve.wait_ge(fin_in[at % FIN_RING], 16 * (at // FIN_RING + 1))
                if at >= FIN_RING:
                    dve.wait_ge(fin_rstd, 2 * (at - FIN_RING + 1))
                for t in range(TT):
                    nc.vector.bn_stats(stats2[:, t, :], fin[:, at % FIN_RING, t, :]).then_inc(fin_step, 1)
                dve.wait_ge(fin_step, 2 * TT * at + TT)
                for t in range(TT):
                    nc.vector.bn_aggr(mv2[:, at % FIN_RING, t, :], stats2[:, t, :]).then_inc(fin_step, 1)
                dve.wait_ge(fin_step, 2 * TT * (at + 1))
                nc.vector.tensor_scalar_add(ve2[:, at % FIN_RING, :], mv2[:, at % FIN_RING, :, 1], EPS).then_inc(fin_var, 1)
                nc.vector.tensor_scalar_mul(nmean[:, at % FIN_RING, :], mv2[:, at % FIN_RING, :, 0], -1.0).then_inc(fin_var, 1)

    @block.tensor
    def _(pe):
        for stage, q, n in expert_steps():
            e, tiles, cols = job(q) if stage in ("turn", "up", "down") else (0, (), 0)
            if stage == "turn":
                pe.wait_ge(tok_in[q % TOK_RING], 48 * (q // TOK_RING + 1))
                for k in range(KC):
                    if q:
                        pe.wait_ge(tp_lo, KC * (q - 1) + k + 1)
                    for at, j in enumerate(tiles):
                        rows = rows_of(j)
                        ins = nc.tensor.transpose(tp_ps[k][:, at * P:at * P + rows], tok[q % TOK_RING][0:rows, at, k * P:(k + 1) * P],
                                                  ident[0:rows, 0:rows])
                    ins.then_inc(tp_done, 1)
            elif stage == "rows":
                for t in range(TT):
                    ins = nc.tensor.transpose(pick_ps[0:late, t * P:(t + 1) * P], scores[:, t, EARLY:B, :].rearrange("p b e -> p (b e)"),
                                              ident[:, :])
                ins.then_inc(rows_ready, 1)
            elif stage == "picked":
                pe.wait_ge(best_ready, 1)
                nc.tensor.transpose(pick_ps[:, 0:late], best_f[:, 0:P], ident[0:late, 0:late])
                nc.tensor.transpose(pick_ps[:, late:2 * late], best[:, 0:P], ident[0:late, 0:late]).then_inc(best_t, 1)
            elif stage == "up":
                at = KH * q + n
                if n == 0:
                    pe.wait_ge(tp_hi, KC * (q + 1))
                    pe.wait_ge(tp_lo, KC * (q + 1))
                    pe.wait_ge(w1_cut, e + 1)
                if at >= H_RING:
                    pe.wait_ge(g_done, at - H_RING + 1)
                units = slice(n * P, (n + 1) * P)
                terms = [(w, x, k) for w, x in ((w1_hi, tt_hi), (w1_hi, tt_lo), (w1_lo, tt_hi)) for k in range(KC)]
                for i, (w, x, k) in enumerate(terms):
                    ins = nc.tensor.matmul(h_ps[at % H_RING][:, 0:cols], w[:, e % 2, k, units], x[:, q % TOK_RING, k, 0:cols],
                                           start=i == 0, stop=i == len(terms) - 1)
                ins.then_inc(h_done, 1)
            elif stage == "down":
                at, rows = 3 * q + n, rows_of(tiles[n])
                if n == 0:
                    pe.wait_ge(g_hi, KH * (q + 1))
                    pe.wait_ge(g_lo, KH * (q + 1))
                    pe.wait_ge(w2_cut, e + 1)
                if at >= Y_RING:
                    pe.wait_ge(y_out, at - Y_RING + 1)
                toks = slice(n * P, n * P + rows)
                terms = [(x, w, m) for m in range(KH) for x, w in ((h_hi, w2_hi), (h_lo, w2_hi), (h_hi, w2_lo))]
                for i, (x, w, m) in enumerate(terms):
                    ins = nc.tensor.matmul(y_ps[at % Y_RING][0:rows, 0:C], x[:, q % 2, m, toks], w[:, e % 2, m, :],
                                           start=i == 0, stop=i == len(terms) - 1)
                ins.then_inc(y_done, 1)


def build(nc, xt_d, x_d, wqkv_d, wp_d, rw_d, w1_d, b1_d, w2_d, b2_d, out_d):
    x1_d = nc.dram_tensor("x1", [B * T, C], F32).ap()
    acc_d = nc.dram_tensor("acc", [B * T, C], F32).ap()
    with ExitStack() as both:
        def sb(name, shape, dt):
            return both.enter_context(nc.sbuf_tensor(name, shape, dt))

        ident = sb("ident", [P, P], F32)
        scores = sb("scores", [P, TT, B, E], F32)
        chosen = {
            "tok_no": sb("tok_no", [P, B, E], U32),
            "gate": sb("gate", [P, B, E], F32),
            "left_f": sb("left_f", [B, E], F32),
            "left_gate": sb("left_gate", [B, E], F32),
        }
        ahead = {
            "w1_raw": sb("w1_raw", [P, KC, HID], F32),
            "w2_raw": sb("w2_raw", [P, KH, C], F32),
            "tok0": sb("tok0", [P, 3, C], F32),
            "tok1": sb("tok1", [P, 3, C], F32),
            "w1_in": both.enter_context(nc.semaphore("w1_in")),
            "w2_in": both.enter_context(nc.semaphore("w2_in")),
            "tok_in0": both.enter_context(nc.semaphore("tok_in0")),
            "tok_in1": both.enter_context(nc.semaphore("tok_in1")),
        }
        with ExitStack() as ctx:
            attention(nc, ctx, xt_d, x_d, wqkv_d, wp_d, rw_d, x1_d, acc_d, ident, scores, chosen, w1_d, w2_d, ahead)
        with ExitStack() as ctx:
            experts(nc, ctx, x1_d, acc_d, w1_d, b1_d, w2_d, b2_d, out_d, ident, scores, chosen, ahead)


def kernel(L0_attn_x, L0_attn_W_key, L0_attn_W_query, L0_attn_W_value, L0_attn_W_proj,
           L0_ffn_router_w, L0_ffn_w1, L0_ffn_b1, L0_ffn_w2, L0_ffn_b2):
    import concourse.bacc as bacc
    from concourse.bass_utils import run_bass_kernel_spmd

    x = np.asarray(L0_attn_x).reshape(B * T, C)
    wqkv = np.concatenate([np.asarray(L0_attn_W_query).T, np.asarray(L0_attn_W_key).T, np.asarray(L0_attn_W_value).T], axis=1)
    arrays = {
        "in_xt": x.T,
        "in_x": x,
        "in_wqkv": wqkv,
        "in_wp": np.asarray(L0_attn_W_proj).T,
        "in_rw": np.asarray(L0_ffn_router_w).T,
        "in_w1": np.asarray(L0_ffn_w1),
        "in_b1": np.asarray(L0_ffn_b1).reshape(E, KH, P).transpose(2, 0, 1).reshape(P, E * KH),
        "in_w2": np.asarray(L0_ffn_w2),
        "in_b2": np.asarray(L0_ffn_b2),
    }
    arrays = {n: np.ascontiguousarray(a) for n, a in arrays.items()}
    nc = bacc.Bacc("TRN2", target_bir_lowering=False, num_devices=1)
    args = [nc.dram_tensor(n, a.shape, mybir.dt.from_np(a.dtype), kind="ExternalInput").ap() for n, a in arrays.items()]
    out = nc.dram_tensor("out_0", (B * T, C), F32, kind="ExternalOutput").ap()
    build(nc, *args, out)
    r = run_bass_kernel_spmd(nc, [arrays], core_ids=[0])
    return r.results[0]["out_0"].reshape(B, T, C)
```

```python
import numpy as np
import concourse.bass as bass
from concourse import mybir
from contextlib import ExitStack

F32 = mybir.dt.float32
F32R = mybir.dt.float32r
BF16 = mybir.dt.bfloat16
I32 = mybir.dt.int32
U32 = mybir.dt.uint32
ALU = mybir.AluOpType
ACT = mybir.ActivationFunctionType
AX = mybir.AxisListType

P = 128
B, T, C = 8, 512, 256
H, D = 16, 16
E, HID = 8, 1024
CAP = int(T * 2.0 / E) + 1
KC = C // P
TT = T // P
KH = HID // P
PAIRS = H // 2
GROUPS = H // 4
VW = 32
BIG_NEG = -1.0e30
EPS = 1e-5
S_SCALE = float(C) ** -1 * float(D) ** -0.5
O_SCALE = float(C) ** -0.5 * float(C) ** -0.5

K_PARTS = (0, 0, 1, 1, 0, 2)
Q_PARTS = (0, 1, 0, 1, 2, 0)
K_RUNS = ((0, 2, 0, 0), (2, 2, 1, 0), (4, 2, 0, 2))
Q_RUNS = ((0, 2, 0, 1), (2, 2, 0, 1), (4, 1, 2, 0), (5, 1, 0, 0))
KQ = len(K_PARTS) * D
KM = KQ + 3

ST_UNITS = (((0, 0, 0),), ((0, 1, 0), (0, 3, 384)), ((0, 2, 0), (1, 2, 256)), ((1, 0, 0),), ((1, 1, 0), (1, 3, 384)))
UP = len(ST_UNITS)
ST_AT = {(h, kb): (u, c) for u, unit in enumerate(ST_UNITS) for h, kb, c in unit}
N_UNITS = [(qb, h - heads + 1, heads) for h in range(H) for qb, heads in ((3, 1), (2, 1), (1, 2), (0, 4)) if (h + 1) % heads == 0]
NU = len(N_UNITS)
N_QUARTER = NU // 4
ST_RING, N_RING, PT_RING = 2, 3, 4

STAGES = (
    (0, 1, 'stack', 1, 1),
    (0, 2, 'res', 0, 0),
    (0, 2, 'qk', 2, 0),
    (0, 8, 'onorm', -1, 2),
    (1, 0, 'qk', 2, 1),
    (1, 0, 'onorm', -1, 3),
    (1, 5, 'ot', -1, 0),
    (1, 6, 'ot', -1, 1),
    (1, 7, 'qk', 2, 2),
    (1, 9, 'proj', -1, 0),
    (1, 9, 'proj', -1, 1),
    (2, 1, 'stack', 2, 0),
    (2, 2, 'qk', 2, 3),
    (2, 4, 'onorm', 0, 0),
    (2, 5, 'x1', -1, 0),
    (2, 5, 'v', 2, 0),
    (2, 7, 'v', 2, 1),
    (2, 9, 'x1t', -1, 0),
    (3, 0, 'nmcut', 1, 0),
    (3, 1, 'x1t', -1, 1),
    (3, 3, 'nm', 1, 0),
    (3, 3, 'onorm', 0, 1),
    (3, 4, 'logit', -1, 0),
    (3, 5, 'split', 3, 0),
    (3, 9, 'score', -1, 0),
)
EARLY = 6
ROUNDS = -(-CAP // 8)
CUTS_AT = ((B, 1), (B, 12))
ROUND_AT = [(B - 1, place) for place in (1, 2, 8, 11, 12, 16, 17, 23, 25, 26, 32, 38, 39)]
ROUND_AT += [(B, place) for place in (1, 5, 12, 16)]
STARTED = [(-2, stage, n) for stage in ("qk", "v", "stack") for n in range(4)]
STARTED += [(-1, "stack", 0), (-1, "nmcut", 0), (-1, "nm", 0)]
AV_PLACES = (4, 5, 6, 7)
BY_ACT = ("qk", "v", "nm", "ot", "x1t")
BY_DVE = ("onorm", "proj", "logit", "pick", "picked")


def steps():
    for i in range(-3, B + 1):
        for g in range(4):
            nat_b, nat_0 = (i + 2, 0) if g == 3 else (i + 1, (g + 1) * N_QUARTER)
            for k in range(10):
                if (i, g, k) == (-1, 3, 0):
                    yield "nmcut", 0, 0
                    yield "nm", 0, 0
                if 0 <= i < B:
                    yield "st", i, (2 * g) * UP + k
                if 0 <= nat_b < B:
                    for n in range(N_QUARTER * k // 10, N_QUARTER * (k + 1) // 10):
                        yield "nat", nat_b, nat_0 + n
                group = i * GROUPS + g - 1
                if k in AV_PLACES and 0 <= group < B * GROUPS:
                    yield "av", group, AV_PLACES.index(k)
                if (i, g, k) == (-2, 0, 0):
                    for stage, n in (("qk", 0), ("qk", 1), ("stack", 0), ("v", 0), ("qk", 2), ("qk", 3), ("v", 1)):
                        yield stage, 0, n
                for gg, kk, stage, ahead, n in STAGES:
                    if (gg, kk) == (g, k) and 0 <= i + ahead < B and (i, stage, n) not in STARTED:
                        yield stage, i + ahead, n
                        if (i, stage, n) == (-1, "qk", 1):
                            yield "stack", 1, 0
                place = 10 * g + k
                if (i, place) == (B - 1, 1):
                    yield "pick", 0, 0
                if (i, place) in ROUND_AT:
                    yield "round", 0, ROUND_AT.index((i, place))
                if (i, place) in CUTS_AT:
                    yield "cut", 0, CUTS_AT.index((i, place))
                if (i, place) == (B, 17):
                    yield "picked", 0, 0
                    yield "fetch", 0, 0


def numbers(stages):
    return {x: n for n, x in enumerate(x for x in steps() if x[0] in stages)}


def pick_round(nc, link, pool, best, at, r):
    src, eight = pool[r % 2], slice(8 * r, 8 * r + 8)
    link(nc.vector.max(best[:, eight], src[:, :]))
    link(nc.vector.max_index(at[:, eight], best[:, eight], src[:, :]))
    if r + 1 < ROUNDS:
        link(nc.vector.match_replace(pool[(r + 1) % 2][:, :], best[:, eight], src[:, :], -1.0))


def weight_parts(ahead, name, slot):
    m, n = (KC, HID) if name == "w1" else (KH, C)
    both = ahead[name][:, slot, :].bitcast(F32R).rearrange("p (i m n) -> p i m n", i=2, m=m)
    return both[:, 0, :, :], both[:, 1, :, :]


def attention(nc, ctx, xt_d, x_d, wqkv_d, wp_d, rw_d, x1_d, acc_d, ident, scores, chosen, w1_d, w2_d, ahead):
    def sb(name, shape, dt):
        return ctx.enter_context(nc.sbuf_tensor(name, shape, dt))

    def pb(name, shape, dt=F32):
        return ctx.enter_context(nc.psum_tensor(name, shape, dt))

    def sem(name):
        return ctx.enter_context(nc.semaphore(name))

    w_hi = sb("w_hi", [P, KC, 3 * C], F32R)
    w_lo = sb("w_lo", [P, KC, 3 * C], F32R)
    wp = sb("wp", [P, KC, C], F32)
    rw = sb("rw", [P, KC, E], F32)
    ident_b = sb("ident_b", [P, P], BF16)
    tri = sb("tri", [P, 4, P], BF16)
    xt = ahead["w1_raw"][:, 0, :].rearrange("p (k n) -> p k n", k=KC)
    qk_f = ahead["w1_raw"][:, 1, :].rearrange("p (a n) -> p a n", a=2)
    w2_flat = ahead["w2_raw"][:, :, :].rearrange("p m c -> p (m c)")
    parts = w2_flat[:, 0:3 * T].bitcast(BF16).rearrange("p (a i n) -> p a i n", a=2, i=3)
    qk_r = w2_flat[:, 3 * T:4 * T]
    xt_hi = sb("xt_hi", [P, KC, T], F32R)
    xt_lo = sb("xt_lo", [P, KC, T], F32R)
    kst = ahead["w1"][0:KM, :, :].bitcast(BF16).rearrange("p a (h n) -> p a h n", h=H)
    qst = ahead["w2"][0:KM, :, :].bitcast(BF16).rearrange("p a (h n) -> p a h n", h=H)
    vaug = sb("vaug", [P, 3, TT, H, VW], F32)
    nmax = sb("nmax", [P, 2, TT, H], F32)
    nmax_r = sb("nmax_r", [P, TT, H], F32)
    nm3 = sb("nm3", [P, TT, 3, H], BF16)
    nmt = sb("nmt", [3 * H, T], BF16)
    pt = sb("pt", [P, PT_RING, UP, T], F32)
    av_sb = sb("av_sb", [P, 2, T], F32)
    rden = sb("rden", [P, TT, 4], F32)
    o_nat = sb("o_nat", [P, TT, C], F32)
    o_t = sb("o_t", [P, KC, T], F32)
    res = sb("res", [P, 2, TT, C], F32)
    stats = sb("stats", [P, TT, 6], F32)
    mv = sb("mv", [P, TT, 2], F32)
    ve = sb("ve", [P, TT], F32)
    half = sb("half", [P, TT], F32)
    rstd = sb("rstd", [P, TT], F32)
    x1t = sb("x1t", [P, KC, T], F32)
    lg = sb("lg", [P, TT, E], F32)
    lge = sb("lge", [P, TT, E], F32)
    lmax = sb("lmax", [P, TT], F32)
    lsum = sb("lsum", [P, TT], F32)
    linv = sb("linv", [P, TT], F32)

    st_ps = [pb(f"st_ps{n}", [P, T]) for n in range(ST_RING)]
    n_ps = [pb(f"n_ps{n}", [P, T]) for n in range(N_RING)]
    av_ps = pb("av_ps", [P, T])
    stage_ps = [pb(f"stage_ps{n}", [P, T]) for n in range(2)]

    early = EARLY * E
    row_pool = [sb(f"row_pool{n}", [early, T], F32) for n in range(2)]
    best = sb("best", [early, 8 * ROUNDS], F32)
    best_at = sb("best_at", [early, 8 * ROUNDS], U32)
    best_f = sb("best_f", [early, 8 * ROUNDS], F32)
    base_i = sb("base_i", [P, EARLY], I32)

    w_in = sem("w_in")
    wp_in = sem("wp_in")
    w_split = sem("w_split")
    pool_step = sem("pool_step")
    consts = sem("consts")
    dve_step = sem("dve_step")
    xt_in = sem("xt_in")
    x_hi = sem("x_hi")
    x_split = sem("x_split")
    res_in = [sem("res_in0"), sem("res_in1")]
    qk_first = sem("qk_first")
    qk_rest = sem("qk_rest")
    parts_out = [sem("parts_out0"), sem("parts_out1")]
    stack_in = [[sem(f"stack{h}{p}") for p in range(2)] for h in range(2)]
    nat_done = sem("nat_done")
    max_done = sem("max_done")
    nm_parts = sem("nm_parts")
    rows_in = sem("rows_in")
    st_done = sem("st_done")
    exp_done = sem("exp_done")
    masked = sem("masked")
    av_done = sem("av_done")
    av_out = sem("av_out")
    act_ready = sem("act_ready")
    act_free = sem("act_free")
    dve_ready = sem("dve_ready")
    dve_free = sem("dve_free")
    var_ready = sem("var_ready")
    rstd_ready = sem("rstd_ready")
    x1_ready = sem("x1_ready")
    x1_out = sem("x1_out")
    lexp = sem("lexp")
    scored = sem("scored")

    best_ready = sem("best_ready")
    left_in = sem("left_in")
    bases = sem("bases")

    part_d = nc.dram_tensor("part_d", [2, 2, 3, D, H, T], BF16).ap()

    act_no, dve_no = numbers(BY_ACT), numbers(BY_DVE)

    banked = [x for x in steps() if x[0] in BY_ACT + BY_DVE]
    turn_no = {x: n for n, x in enumerate(banked)}

    def is_first(stage, b):
        return stage in ("qk", "v") and b == 0

    def stage_bank(stage, b, n):
        return st_ps[act_no[(stage, b, n)] % ST_RING] if is_first(stage, b) else stage_ps[turn_no[(stage, b, n)] % 2]

    block = ctx.enter_context(nc.Block())

    @block.sync
    def _(sp):
        def load_xt(b):
            sp.dma_start(xt[:, :, :], xt_d[:, b * T:(b + 1) * T].rearrange("(k p) n -> p k n", p=P)).then_inc(xt_in, 16)

        sp.dma_start(pt[:, 0, 0:3, :], wqkv_d.rearrange("(k p) n -> p k n", p=P)).then_inc(w_in, 16)
        load_xt(0)
        sp.dma_start(wp[:, :, :], wp_d.rearrange("(k p) n -> p k n", p=P)).then_inc(wp_in, 16)
        sp.dma_start(rw[:, :, :], rw_d.rearrange("(k p) n -> p k n", p=P)).then_inc(wp_in, 16)
        for stage, b, n in steps():
            if stage == "split" and b + 1 < B:
                sp.wait_ge(x_split, b + 1)
                load_xt(b + 1)
            elif stage == "res":
                if b >= 2:
                    sp.wait_ge(x1_out, 32 * (b - 1))
                    sp.wait_ge(act_ready, act_no[("x1t", b - 2, 1)] + 1)
                sp.dma_start(res[:, b % 2, :, :], x_d[b * T:(b + 1) * T, :].rearrange("(t p) n -> p t n", p=P)).then_inc(res_in[b % 2], 16)
            elif stage == "qk":
                tile, which, half_ = 4 * b + n, n % 2, n // 2
                sp.wait_ge(qk_first, tile + 1)
                sp.wait_ge(qk_rest, tile + 1)
                if b >= 2:
                    sp.wait_ge(stack_in[half_][b % 2], 16 * (len(K_RUNS) + len(Q_RUNS)) * (b // 2))
                for part in range(3):
                    dst = part_d[which, b % 2, part, :, 8 * half_:8 * half_ + 8, :]
                    sp.dma_start(dst.rearrange("d h n -> h d n"), parts[:, tile % 2, part, :]).then_inc(parts_out[tile % 2], 16)
            elif stage == "stack":
                for parity in range(2):
                    sp.wait_ge(parts_out[parity], 48 * (2 * b + n + 1))
                if b >= 2:
                    sp.wait_ge(st_done, ((b - 2) * PAIRS + 4 * (n + 1)) * UP)
                for which, stack, runs in ((0, qst, Q_RUNS), (1, kst, K_RUNS)):
                    for at, count, first, step in runs:
                        src = part_d[which, b % 2, first:first + 1 + step * (count - 1):max(step, 1), :, 8 * n:8 * n + 8, :]
                        if step == 0:
                            src = src.to_broadcast([count, D, 8, T])
                        sp.dma_start(stack[at * D:(at + count) * D, b % 2, 8 * n:8 * n + 8, :],
                                     src.rearrange("i d h n -> i d (h n)")).then_inc(stack_in[n][b % 2], 16)
                if (b, n) == (B - 1, 1):
                    sp.wait_ge(x_split, B)
                    sp.wait_ge(qk_rest, 4 * B)
                    sp.dma_start(ahead["w1_raw"][:, :, :], w1_d[0].rearrange("(k p) n -> p k n", p=P)).then_inc(ahead["w1_in"], 16)
                    sp.dma_start(ahead["w2_raw"][:, :, :], w2_d[0].rearrange("(k p) n -> p k n", p=P)).then_inc(ahead["w2_in"], 16)
            elif stage == "nm":
                sp.wait_ge(act_free, act_no[(stage, b, n)] + 1)
                for at in range(3):
                    sp.dma_start(qst[KQ + at:KQ + at + 1, b % 2, :, :], nmt[at * H:(at + 1) * H, :]).then_inc(rows_in, 16)
            elif stage == "picked":
                sp.wait_ge(best_ready, 1)
                sp.dma_start(chosen["left_f"][0:EARLY, :], best_f[:, P:P + 1]).then_inc(left_in, 16)
                sp.dma_start(chosen["left_gate"][0:EARLY, :], best[:, P:P + 1]).then_inc(left_in, 16)
            elif stage == "x1":
                sp.wait_ge(x1_ready, TT * (b + 1))
                for dst in (x1_d, acc_d):
                    sp.dma_start(dst[b * T:(b + 1) * T, :].rearrange("(t p) n -> p t n", p=P), res[:, b % 2, :, :]).then_inc(x1_out, 16)
        sp.wait_ge(x1_out, 32 * B)
        sp.wait_ge(left_in, 32)
        sp.wait_ge(ahead["w1_in"], 16)
        sp.wait_ge(ahead["w2_in"], 16)

    @block.gpsimd
    def _(pool):
        made = [0]

        def link(ins):
            made[0] += 1
            ins.then_inc(pool_step, 1)
            pool.wait_ge(pool_step, made[0])

        link(nc.gpsimd.memset(ident[:, :], 0.0))
        link(nc.gpsimd.affine_select(out=ident[:, :], in_=ident[:, :], compare_op=ALU.not_equal, fill=1.0, base=0,
                                     pattern=[[-1, P]], channel_multiplier=1))
        nc.gpsimd.tensor_copy(ident_b[:, :], ident[:, :]).then_inc(consts, 1)
        link(nc.gpsimd.memset(tri[:, :, :], 0.0))
        nc.gpsimd.affine_select(out=tri[:, 3, :], in_=tri[:, 3, :], compare_op=ALU.is_ge, fill=BIG_NEG, base=0,
                                pattern=[[-1, P]], channel_multiplier=1).then_inc(consts, 1)
        link(nc.gpsimd.memset(half[:, :], -0.5))
        nc.gpsimd.iota(base_i[:, :], pattern=[[T, EARLY]], base=0, channel_multiplier=0).then_inc(bases, 1)
        for stage, b, n in steps():
            if stage == "st":
                pool.wait_ge(exp_done, (b * PAIRS * UP) + n + 1)
                pair, u = n // UP, n % UP
                tiles = [c // P for _, _, c in ST_UNITS[u]]
                x = pt[:, (b * PAIRS + pair) % PT_RING, u, :].rearrange("p (j q) -> p j q", q=P)
                x = x[:, tiles[0]:tiles[-1] + 1:max(1, tiles[-1] - tiles[0]), :]
                nc.gpsimd.affine_select(out=x, in_=x, compare_op=ALU.is_ge, fill=0.0, base=0,
                                        pattern=[[0, len(tiles)], [1, P]], channel_multiplier=-1).then_inc(masked, 1)
            elif stage == "qk" and b:
                tile = 4 * b + n
                pool.wait_ge(qk_first, tile + 1)
                pool.wait_ge(act_free, act_no[(stage, b, n)] + 1)
                pool.wait_ge(qk_rest, tile)
                pool.wait_ge(parts_out[tile % 2], 48 * (tile // 2))
                link(nc.gpsimd.tensor_tensor(qk_r[:, :], qk_f[:, tile % 2, :], parts[:, tile % 2, 0, :], ALU.subtract))
                link(nc.gpsimd.tensor_tensor(parts[:, tile % 2, 1, :], qk_f[:, tile % 2, :], parts[:, tile % 2, 0, :], ALU.subtract))
                nc.gpsimd.tensor_tensor(parts[:, tile % 2, 2, :], qk_r[:, :], parts[:, tile % 2, 1, :], ALU.subtract).then_inc(qk_rest, 1)
            elif stage == "split":
                pool.wait_ge(x_hi, b + 1)
                nc.gpsimd.tensor_tensor(xt_lo[:, :, :], xt[:, :, :], xt_hi[:, :, :].bitcast(F32), ALU.subtract).then_inc(x_split, 1)
                if b == 0:
                    link(nc.gpsimd.memset(vaug[:, :, :, :, D:VW], 0.0))
                    nc.gpsimd.memset(vaug[:, :, :, :, D:D + 1], 1.0).then_inc(consts, 1)
                    pool.wait_ge(consts, 3)
                    two_ones = float(np.array([0x3F803F80], np.uint32).view(np.float32)[0])
                    nc.gpsimd.memset(kst[KQ:KM, :, :, :].rearrange("p a h n -> p (a h n)").bitcast(F32), two_ones).then_inc(consts, 1)
                    pool.wait_ge(consts, 4)
            elif stage == "x1":
                pool.wait_ge(var_ready, b + 1)
                nc.gpsimd.tensor_tensor(rstd[:, :], ve[:, :], half[:, :], ALU.pow).then_inc(rstd_ready, 1)
            elif stage == "cut":
                pool.wait_ge(ahead[("w1_top", "w2_top")[n]], 1)
                hi, lo = weight_parts(ahead, ("w1", "w2")[n], 0)
                nc.gpsimd.tensor_tensor(lo, ahead[("w1_raw", "w2_raw")[n]][:, :, :], hi.bitcast(F32), ALU.subtract).then_inc(ahead[("w1_cut", "w2_cut")[n]], 1)
            elif stage == "fetch":
                pool.wait_ge(dve_free, dve_no[("picked", 0, 0)] + 1)
                pool.wait_ge(x1_out, 32 * EARLY)
                for q in range(2):
                    for at, j in enumerate(CHUNKS[q]):
                        nc.gpsimd.indirect_dma_start(ahead[f"tok{q}"][:, at, :], None, x1_d[0:EARLY * T, :],
                                                     bass.IndirectOffsetOnAxis(ap=chosen["tok_no"][:, j, 0:1], axis=0)).then_inc(ahead[f"tok_in{q}"], 16)

    @block.scalar
    def _(act):
        for stage, b, n in steps():
            if stage in BY_ACT:
                ps = stage_bank(stage, b, n)
                act.wait_ge(act_ready, act_no[(stage, b, n)] + 1)
            if stage == "st":
                at, slot = b * PAIRS * UP + n, b * PAIRS + n // UP
                act.wait_ge(st_done, at + 1)
                if n % UP == 0 and slot >= PT_RING:
                    act.wait_ge(av_done, (slot - PT_RING) // 2 + 1)
                nc.scalar.activation(pt[:, slot % PT_RING, n % UP, :], st_ps[at % ST_RING][:, :], ACT.Exp,
                                     scale=S_SCALE).then_inc(exp_done, 1)
            elif stage == "split":
                act.wait_ge(xt_in, 16 * (b + 1))
                if b >= 1:
                    act.wait_ge(act_ready, act_no[("v", b - 1, 1)] + 1)
                    act.wait_ge(x_split, b)
                nc.scalar.activation(xt_hi[:, :, :], xt[:, :, :], ACT.Copy).then_inc(x_hi, 1)
            elif stage == "cut":
                act.wait_ge(ahead[("w1_in", "w2_in")[n]], 16)
                act.wait_ge(st_done, (B - 1) * PAIRS * UP)
                hi, _ = weight_parts(ahead, ("w1", "w2")[n], 0)
                nc.scalar.activation(hi, ahead[("w1_raw", "w2_raw")[n]][:, :, :], ACT.Copy).then_inc(ahead[("w1_top", "w2_top")[n]], 1)
            elif stage == "av" and n == 3:
                act.wait_ge(av_done, b + 1)
                if b >= 2:
                    last = ("onorm", (b - 2) // GROUPS, (b - 2) % GROUPS)
                    act.wait_ge(dve_ready, dve_no[last] + 1)
                nc.scalar.activation(av_sb[:, b % 2, :], av_ps[:, :], ACT.Copy).then_inc(av_out, 1)
            elif stage == "qk":
                tile = 4 * b + n
                if tile >= 2:
                    act.wait_ge(qk_rest, tile - 1)
                    act.wait_ge(parts_out[tile % 2], 48 * (tile // 2))
                nc.scalar.activation(parts[:, tile % 2, 0, :], ps[:, :], ACT.Copy).then_inc(qk_first, 1)
                nc.scalar.activation(qk_f[:, tile % 2, :], ps[:, :], ACT.Copy).then_inc(act_free, 1)
            elif stage == "v":
                if b == 0 and n == 0:
                    act.wait_ge(consts, 3)
                if b >= 3:
                    act.wait_ge(av_done, (b - 2) * GROUPS)
                src = ps[:, :].rearrange("p (t h d) -> p t h d", t=2, h=H)
                for t in range(2):
                    ins = nc.scalar.activation(vaug[:, b % 3, 2 * n + t, :, 0:D], src[:, t, :, :], ACT.Copy)
                ins.then_inc(act_free, 1)
            elif stage == "nm":
                if b >= 1:
                    act.wait_ge(rows_in, 48 * b)
                nc.scalar.activation(nmt[:, :], ps[:, :].bitcast(BF16)[0:3 * H, 0:T], ACT.Copy).then_inc(act_free, 1)
            elif stage == "ot":
                if b >= 1:
                    act.wait_ge(dve_ready, dve_no[("proj", b - 1, 1)] + 1)
                nc.scalar.activation(o_t[:, n, :], ps[:, :], ACT.Copy).then_inc(act_free, 1)
            elif stage == "x1t":
                if b >= 1:
                    act.wait_ge(dve_ready, dve_no[("logit", b - 1, 0)] + 1)
                nc.scalar.activation(x1t[:, n, :], ps[:, :], ACT.Copy).then_inc(act_free, 1)
            elif stage == "logit":
                act.wait_ge(dve_free, dve_no[(stage, b, n)] + 1)
                if b >= 1:
                    act.wait_ge(scored, b)
                nc.scalar.activation(lge[:, :, :], lg[:, :, :], ACT.Exp).then_inc(lexp, 1)

    @block.vector
    def _(dve):
        made = [0]

        def link(ins):
            made[0] += 1
            ins.then_inc(dve_step, 1)
            dve.wait_ge(dve_step, made[0])

        dve.wait_ge(w_in, 16)
        raw = pt[:, 0, 0:3, :].rearrange("p a n -> p (a n)").rearrange("p (k n) -> p k n", k=KC)
        link(nc.vector.tensor_copy(w_hi[:, :, :], raw))
        nc.vector.tensor_tensor(w_lo[:, :, :], raw, w_hi[:, :, :].bitcast(F32), ALU.subtract).then_inc(w_split, 1)
        for stage, b, n in steps():
            if stage in BY_DVE:
                ps = stage_bank(stage, b, n)
                dve.wait_ge(dve_ready, dve_no[(stage, b, n)] + 1)
                if dve_no[(stage, b, n)]:
                    dve.wait_ge(dve_free, dve_no[(stage, b, n)])
            if stage == "nat":
                qb, h0, heads = N_UNITS[n]
                at = b * NU + n
                dve.wait_ge(nat_done, at + 1)
                if at == 0:
                    dve.wait_ge(consts, 2)
                src = n_ps[at % N_RING][:, 0:heads * (qb + 1) * P].rearrange("p (h k) -> p h k", h=heads)
                mask = tri[:, 3 - qb:4, :].rearrange("p a k -> p (a k)")
                for h in range(heads):
                    ins = nc.vector.tensor_tensor_reduce(out=src[:, h, :], in0=src[:, h, :], in1=mask, scale=-1.0, scalar=-BIG_NEG,
                                                         op0=ALU.add, op1=ALU.min, accum_out=nmax[:, b % 2, qb, h0 + h:h0 + h + 1])
                ins.then_inc(max_done, 1)
            elif stage == "qk" and b == 0:
                dve.wait_ge(qk_first, n + 1)
                dve.wait_ge(act_free, act_no[(stage, b, n)] + 1)
                if n:
                    dve.wait_ge(qk_rest, n)
                if n >= 2:
                    dve.wait_ge(parts_out[n % 2], 48 * (n // 2))
                link(nc.vector.tensor_tensor(qk_r[:, :], qk_f[:, n % 2, :], parts[:, n % 2, 0, :], ALU.subtract))
                link(nc.vector.tensor_tensor(parts[:, n % 2, 1, :], qk_f[:, n % 2, :], parts[:, n % 2, 0, :], ALU.subtract))
                nc.vector.tensor_tensor(parts[:, n % 2, 2, :], qk_r[:, :], parts[:, n % 2, 1, :], ALU.subtract).then_inc(qk_rest, 1)
            elif stage == "nmcut":
                dve.wait_ge(max_done, NU * (b + 1))
                if b >= 1:
                    dve.wait_ge(act_ready, act_no[("nm", b - 1, 0)] + 1)
                link(nc.vector.tensor_copy(nm3[:, :, 0, :], nmax[:, b % 2, :, :]))
                link(nc.vector.tensor_tensor(nmax_r[:, :, :], nmax[:, b % 2, :, :], nm3[:, :, 0, :], ALU.subtract))
                link(nc.vector.tensor_copy(nm3[:, :, 1, :], nmax_r[:, :, :]))
                nc.vector.tensor_tensor(nm3[:, :, 2, :], nmax_r[:, :, :], nm3[:, :, 1, :], ALU.subtract).then_inc(nm_parts, 1)
            elif stage == "onorm":
                src = ps[:, :].rearrange("p (t j v) -> p t j v", t=TT, j=4)
                link(nc.vector.reciprocal(rden[:, :, :], src[:, :, :, D]))
                if b >= 1 and n == 0:
                    dve.wait_ge(act_ready, act_no[("ot", b - 1, 1)] + 1)
                dst = o_nat[:, :, 4 * D * n:4 * D * (n + 1)].rearrange("p t (j d) -> p t j d", j=4)
                nc.vector.tensor_tensor(dst, src[:, :, :, 0:D], rden[:, :, :].unsqueeze(3).to_broadcast([P, TT, 4, D]), ALU.mult).then_inc(dve_free, 1)
            elif stage == "proj":
                if n == 0:
                    dve.wait_ge(res_in[b % 2], 16 * (b // 2 + 1))
                rows = res[:, b % 2, 2 * n:2 * n + 2, :].rearrange("p t c -> p (t c)")
                nc.vector.scalar_tensor_tensor(out=rows, in0=ps[:, :], scalar=O_SCALE, in1=rows,
                                               op0=ALU.mult, op1=ALU.add).then_inc(dve_free, 1)
                dve.wait_ge(dve_free, dve_no[(stage, b, n)] + 1)
                for t in (2 * n, 2 * n + 1):
                    ins = nc.vector.bn_stats(stats[:, t, :], res[:, b % 2, t, :])
                    if t % 2 == 0:
                        ins.then_inc(dve_step, 1)
                        made[0] += 1
                link(ins)
                for t in (2 * n, 2 * n + 1):
                    ins = nc.vector.bn_aggr(mv[:, t, :], stats[:, t, :])
                    if t % 2 == 0:
                        ins.then_inc(dve_step, 1)
                        made[0] += 1
                link(ins)
                if n == 1:
                    nc.vector.tensor_scalar_add(ve[:, :], mv[:, :, 1], EPS).then_inc(var_ready, 1)
            elif stage == "x1":
                dve.wait_ge(rstd_ready, b + 1)
                for t in range(TT):
                    row = res[:, b % 2, t, :]
                    nc.vector.tensor_scalar(row, row, mv[:, t, 0:1], rstd[:, t:t + 1], ALU.subtract, ALU.mult).then_inc(x1_ready, 1)
            elif stage == "logit":
                src = ps[:, 0:TT * E].rearrange("p (t e) -> p t e", t=TT)
                link(nc.vector.tensor_reduce(out=lmax[:, :], in_=src, axis=AX.X, op=ALU.max))
                if b >= 1:
                    dve.wait_ge(lexp, b)
                nc.vector.tensor_tensor(lg[:, :, :], src, lmax[:, :].unsqueeze(2).to_broadcast([P, TT, E]), ALU.subtract).then_inc(dve_free, 1)
            elif stage == "pick":
                nc.vector.tensor_copy(row_pool[0][:, :], ps[0:early, :]).then_inc(dve_free, 1)
                dve.wait_ge(dve_free, dve_no[(stage, b, n)] + 1)
            elif stage == "round":
                pick_round(nc, link, row_pool, best, best_at, n)
                if n == ROUNDS - 1:
                    nc.vector.tensor_copy(best_f[:, :], best_at[:, :]).then_inc(best_ready, 1)
            elif stage == "picked":
                dve.wait_ge(bases, 1)
                src = ps[:, 0:2 * early].rearrange("p (a b e) -> p a b e", a=2, b=EARLY)
                link(nc.vector.tensor_tensor(chosen["tok_no"][:, 0:EARLY, :], src[:, 0, :, :],
                                             base_i[:, :].unsqueeze(2).to_broadcast([P, EARLY, E]), ALU.add))
                nc.vector.tensor_copy(chosen["gate"][:, 0:EARLY, :], src[:, 1, :, :]).then_inc(dve_free, 1)
            elif stage == "score":
                dve.wait_ge(lexp, b + 1)
                link(nc.vector.tensor_reduce(out=lsum[:, :], in_=lge[:, :, :], axis=AX.X, op=ALU.add))
                link(nc.vector.reciprocal(linv[:, :], lsum[:, :]))
                nc.vector.tensor_tensor(scores[:, :, b, :], lge[:, :, :], linv[:, :].unsqueeze(2).to_broadcast([P, TT, E]), ALU.mult).then_inc(scored, 1)

    @block.tensor
    def _(pe):
        pe.wait_ge(w_split, 1)
        for stage, b, n in steps():
            if stage in BY_ACT + BY_DVE:
                ps = stage_bank(stage, b, n)
                if is_first(stage, b):
                    if act_no[(stage, b, n)] >= ST_RING:
                        pe.wait_ge(act_free, act_no[(stage, b, n)] - ST_RING + 1)
                elif turn_no[(stage, b, n)] >= 2:
                    before = banked[turn_no[(stage, b, n)] - 2]
                    if before[0] in BY_ACT:
                        pe.wait_ge(act_free, act_no[before] + 1)
                    else:
                        pe.wait_ge(dve_free, dve_no[before] + 1)
            if stage == "st":
                at = b * PAIRS * UP + n
                pair, u = n // UP, n % UP
                if b == 0 and n == 0:
                    pe.wait_ge(consts, 4)
                if n == 0:
                    pe.wait_ge(rows_in, 48 * (b + 1))
                if at >= ST_RING:
                    pe.wait_ge(exp_done, at - ST_RING + 1)
                for hh, kb, c in ST_UNITS[u]:
                    h = 2 * pair + hh
                    ins = nc.tensor.matmul(st_ps[at % ST_RING][:, c:c + T - kb * P], kst[0:KM, b % 2, h, kb * P:(kb + 1) * P],
                                           qst[0:KM, b % 2, h, kb * P:T], start=True, stop=True)
                ins.then_inc(st_done, 1)
            elif stage == "nat":
                qb, h0, heads = N_UNITS[n]
                at = b * NU + n
                if b == 0 and n == 0:
                    pe.wait_ge(consts, 1)
                if n % (NU // 2) == 0:
                    pe.wait_ge(stack_in[n // (NU // 2)][b % 2], 16 * (len(K_RUNS) + len(Q_RUNS)) * (b // 2 + 1))
                if at >= N_RING:
                    pe.wait_ge(max_done, at - N_RING + 1)
                bank, w = n_ps[at % N_RING], (qb + 1) * P
                for j in range(heads):
                    h = h0 + j
                    ins = nc.tensor.matmul(bank[:, j * w:(j + 1) * w], qst[0:KQ, b % 2, h, qb * P:(qb + 1) * P],
                                           kst[0:KQ, b % 2, h, 0:w], start=True, stop=True)
                ins.then_inc(nat_done, 1)
            elif stage == "av":
                seq, group = b // GROUPS, b % GROUPS
                if n == 0:
                    pe.wait_ge(masked, (2 * b + 2) * UP)
                    if b:
                        pe.wait_ge(av_out, b)
                    if group == 0:
                        pe.wait_ge(act_free, act_no[("v", seq, 1)] + 1)
                for j in range(4):
                    h = 4 * group + j
                    u, c = ST_AT[(h % 2, n)]
                    ins = nc.tensor.matmul(av_ps[VW * j:VW * (j + 1), n * P:T], vaug[:, seq % 3, n, h, :],
                                           pt[:, (seq * PAIRS + h // 2) % PT_RING, u, c:c + T - n * P], start=n == 0, stop=n == TT - 1,
                                           skip_group_check=True)
                if n == TT - 1:
                    ins.then_inc(av_done, 1)
            elif stage == "onorm":
                group = b * GROUPS + n
                pe.wait_ge(av_out, group + 1)
                for t in range(TT):
                    ins = nc.tensor.transpose(ps[:, t * P:(t + 1) * P], av_sb[:, group % 2, t * P:(t + 1) * P], ident[:, :])
                ins.then_inc(dve_ready, 1)
            elif stage == "qk":
                which, half_ = n % 2, n // 2
                pe.wait_ge(x_split, b + 1)
                cols = slice(which * C + half_ * P, which * C + half_ * P + P)
                for at, (w, x) in enumerate(((w_hi, xt_hi), (w_hi, xt_lo), (w_lo, xt_hi))):
                    for k in range(KC):
                        ins = nc.tensor.matmul(ps[:, :], w[:, k, cols], x[:, k, :], start=at + k == 0, stop=at == 2 and k == KC - 1)
                ins.then_inc(act_ready, 1)
            elif stage == "v":
                for t in range(2):
                    toks = slice((2 * n + t) * P, (2 * n + t + 1) * P)
                    for at, (w, x) in enumerate(((w_hi, xt_hi), (w_hi, xt_lo), (w_lo, xt_hi))):
                        for k in range(KC):
                            ins = nc.tensor.matmul(ps[:, t * C:(t + 1) * C], x[:, k, toks], w[:, k, 2 * C:3 * C],
                                                   start=at + k == 0, stop=at == 2 and k == KC - 1)
                ins.then_inc(act_ready, 1)
            elif stage == "nm":
                pe.wait_ge(nm_parts, b + 1)
                for t in range(TT):
                    ins = nc.tensor.transpose(ps[:, :].bitcast(BF16)[0:3 * H, t * P:(t + 1) * P], nm3[:, t, :, :].rearrange("p i h -> p (i h)"), ident_b[:, :])
                ins.then_inc(act_ready, 1)
            elif stage == "ot":
                pe.wait_ge(dve_free, dve_no[("onorm", b, 3)] + 1)
                for t in range(TT):
                    ins = nc.tensor.transpose(ps[:, t * P:(t + 1) * P], o_nat[:, t, n * P:(n + 1) * P], ident[:, :])
                ins.then_inc(act_ready, 1)
            elif stage == "proj":
                if b == 0 and n == 0:
                    pe.wait_ge(wp_in, 32)
                pe.wait_ge(act_free, act_no[("ot", b, 1)] + 1)
                for t in range(2):
                    toks = slice((2 * n + t) * P, (2 * n + t + 1) * P)
                    for k in range(KC):
                        ins = nc.tensor.matmul(ps[:, t * C:(t + 1) * C], o_t[:, k, toks], wp[:, k, :], start=k == 0, stop=k == KC - 1)
                ins.then_inc(dve_ready, 1)
            elif stage == "x1t":
                pe.wait_ge(x1_ready, TT * (b + 1))
                for t in range(TT):
                    ins = nc.tensor.transpose(ps[:, t * P:(t + 1) * P], res[:, b % 2, t, n * P:(n + 1) * P], ident[:, :])
                ins.then_inc(act_ready, 1)
            elif stage == "pick":
                pe.wait_ge(scored, EARLY)
                for t in range(TT):
                    ins = nc.tensor.transpose(ps[0:early, t * P:(t + 1) * P],
                                              scores[:, t, 0:EARLY, :].rearrange("p b e -> p (b e)"), ident[:, :])
                ins.then_inc(dve_ready, 1)
            elif stage == "picked":
                pe.wait_ge(best_ready, 1)
                nc.tensor.transpose(ps[:, 0:early], best_f[:, 0:P], ident[0:early, 0:early])
                nc.tensor.transpose(ps[:, early:2 * early], best[:, 0:P], ident[0:early, 0:early]).then_inc(dve_ready, 1)
            elif stage == "logit":
                pe.wait_ge(act_free, act_no[("x1t", b, 1)] + 1)
                for t in range(TT):
                    for k in range(KC):
                        ins = nc.tensor.matmul(ps[:, t * E:(t + 1) * E], x1t[:, k, t * P:(t + 1) * P], rw[:, k, :],
                                               start=k == 0, stop=k == KC - 1)
                ins.then_inc(dve_ready, 1)


LEFT = B
CHUNKS = ((0, 1, 2), (3, 4, 5), (6, 7, LEFT))
NC = len(CHUNKS)
LATE = B - EARLY
JOBS = [(0, 0), (0, 1), (1, 0), (1, 1), (0, 2), (1, 2)] + [(e, c) for e in range(2, E - 1) for c in range(NC)]
JOBS += [(E - 1, c) for c in (2, 0, 1)]
NQ = len(JOBS)
H_RING, Y_RING, TOK_RING, G_RING = 3, 2, 3, 3
TURN_AT, FETCH_AT = 6, 5
SECOND_AT = ((0, 3), (0, 4))
LO_BY_POOL = 1
PICKED_AT = (2, 3)
ROUNDS_IN = (5, 6, 6)
DOWN_AT = (2, 5, 8)


def rows_of(tile):
    return B if tile == LEFT else P


def job(q):
    e, c = JOBS[q]
    return e, CHUNKS[c], sum(rows_of(j) for j in CHUNKS[c])


FIRST_JOB = {e: min(q for q in range(NQ) if JOBS[q][0] == e) for e in range(E)}
LAST_JOB = {e: max(q for q in range(NQ) if JOBS[q][0] == e) for e in range(E)}


FINISH = [((NQ - 2, 0), "load", 6), ((NQ - 2, 1), "load", 7), ((NQ - 2, 4), "norm", 6), ((NQ - 2, 7), "norm", 7),
          ((NQ - 1, 0), "load", 0), ((NQ - 1, 1), "load", 1), ((NQ - 1, 3), "load", 2), ((NQ - 1, 4), "norm", 0),
          ((NQ - 1, 5), "load", 3), ((NQ - 1, 8), "load", 4), ((NQ - 1, 9), "load", 5)]
FINISH += [((NQ - 1, 9), "norm", b) for b in range(1, 6)]
FIN_NO = {b: n for n, b in enumerate(b for _, stage, b in FINISH if stage == "load")}
FIN_OWN = 4


def cut_at(stage, e):
    if e == 1:
        return SECOND_AT[stage == "cut2"]
    if stage == "cut1":
        return FIRST_JOB[e] - 2, 1
    return max(FIRST_JOB[e] - 2, LAST_JOB[e - 2] + 1 if e >= 2 else 0), 4


def expert_steps():
    rounds = 0
    yield "turn", 0, 0
    yield "rows", 0, 0
    for q in range(-1, NQ):
        for m in range(KH + 2):
            if q + 1 < NQ and m < KH:
                yield "up", q + 1, m
            for e in range(1, E):
                for stage in ("cut1", "cut2"):
                    if (q, m) == cut_at(stage, e):
                        yield stage, e, 0
            if q + 1 < len(ROUNDS_IN) and (m + 1) * ROUNDS_IN[q + 1] // (KH + 1) > m * ROUNDS_IN[q + 1] // (KH + 1):
                yield "round", 0, rounds
                rounds += 1
            for at, stage, b in FINISH:
                if (q, m) == at:
                    yield stage, b, 0
            if (q, m) == PICKED_AT:
                yield "picked", 0, 0
            if m == (1 if q < 0 else TURN_AT) and q + 2 < NQ:
                yield "turn", q + 2, 0
            if m == FETCH_AT and TOK_RING <= q + 3 < NQ:
                yield "fetch", q + 3, 0
            if q >= 0 and m in DOWN_AT:
                yield "down", q, m // 3


def adds_before():
    out = {}
    for q, (e, c) in enumerate(JOBS):
        for j in CHUNKS[c]:
            out[q, j] = {}
            for x in range(B + 1) if j == LEFT else (j, LEFT):
                adders = [JOBS[qq][0] for qq in range(q) if x in CHUNKS[JOBS[qq][1]]]
                out[q, j][x] = max([n + 1 for n, adder in enumerate(adders) if adder != e], default=0)
    return out


ADDS = adds_before()


def experts(nc, ctx, x1_d, acc_d, w1_d, b1_d, w2_d, b2_d, out_d, ident, scores, chosen, ahead):
    def sb(name, shape, dt):
        return ctx.enter_context(nc.sbuf_tensor(name, shape, dt))

    def sem(name):
        return ctx.enter_context(nc.semaphore(name))

    late = LATE * E
    tok_no, gate, left_f, left_gate = (chosen[n] for n in ("tok_no", "gate", "left_f", "left_gate"))
    row_pool = [sb(f"late_pool{n}", [late, T], F32) for n in range(2)]
    best = sb("late_best", [late, 8 * ROUNDS], F32)
    best_at = sb("late_best_at", [late, 8 * ROUNDS], U32)
    best_f = sb("late_best_f", [late, 8 * ROUNDS], F32)
    base_i = sb("late_base_i", [P, LATE, E], I32)
    lbase_i = sb("lbase_i", [B, E], I32)
    left_no = sb("left_no", [B, E], U32)
    b1 = sb("b1", [P, E, KH], F32)
    b2 = sb("b2", [P, E, C], F32)
    w1_raw, w2_raw = ahead["w1_raw"], ahead["w2_raw"]
    w1_hi, w1_lo = zip(*(weight_parts(ahead, "w1", slot) for slot in range(2)))
    w2_hi, w2_lo = zip(*(weight_parts(ahead, "w2", slot) for slot in range(2)))
    tok = [ahead["tok0"], ahead["tok1"]] + [sb(f"tok{n}", [P, 3, C], F32) for n in range(2, TOK_RING)]
    tt_hi = sb("tt_hi", [P, TOK_RING, KC, 3 * P], F32R)
    tt_lo = sb("tt_lo", [P, TOK_RING, KC, 3 * P], F32R)
    g = sb("g", [P, G_RING, 3 * P], F32)
    h_hi = sb("h_hi", [P, 2, KH, 3 * P], F32R)
    h_lo = sb("h_lo", [P, 2, KH, 3 * P], F32R)
    y = sb("y", [P, B + 1, C], F32)
    fin_own = sb("fin", [P, FIN_OWN, TT, C], F32)
    fin = [fin_own[:, n, :, :] for n in range(FIN_OWN)]
    for raw in (w1_raw[:, :, :].rearrange("p k n -> p (k n)"), w2_raw[:, :, :].rearrange("p m n -> p (m n)")):
        fin += [raw[:, n * TT * C:(n + 1) * TT * C].rearrange("p (t n) -> p t n", t=TT) for n in range(2)]
    stats2 = sb("stats2", [P, TT, 6], F32)
    mv2 = sb("mv2", [P, B, TT, 2], F32)
    ve2 = sb("ve2", [P, B, TT], F32)
    nmean = sb("nmean", [P, B, TT], F32)
    half2 = sb("half2", [P, TT], F32)
    rstd2 = sb("rstd2", [P, B, TT], F32)
    shift2 = sb("shift2", [P, B, TT], F32)

    h_ps = [ctx.enter_context(nc.psum_tensor(f"h_ps{n}", [P, T], F32)) for n in range(H_RING)]
    y_ps = [ctx.enter_context(nc.psum_tensor(f"y_ps{n}", [P, T], F32)) for n in range(Y_RING)]
    tp_ps = [ctx.enter_context(nc.psum_tensor(f"tp_ps{n}", [P, T], F32)) for n in range(KC)]
    pick_ps = ctx.enter_context(nc.psum_tensor("pick_ps", [P, T], F32))

    rows_ready = sem("rows_ready")
    rows_taken = sem("rows_taken")
    dve_step2 = sem("dve_step2")
    bases = sem("bases2")
    best_ready = sem("best_ready2")
    best_t = sem("best_t")
    left_in = sem("left_in2")
    picked = sem("picked")
    bias_in = sem("bias_in")
    w1_in, w2_in = ahead["w1_in"], ahead["w2_in"]
    w1_top, w2_top = ahead["w1_top"], ahead["w2_top"]
    w1_cut, w2_cut = ahead["w1_cut"], ahead["w2_cut"]
    tok_in = [ahead["tok_in0"], ahead["tok_in1"]] + [sem(f"tok_in{n}") for n in range(2, TOK_RING)]
    tp_done = sem("tp_done")
    tp_hi = sem("tp_hi")
    tp_lo = sem("tp_lo")
    h_done = sem("h_done")
    g_done = sem("g_done")
    g_hi, g_lo = sem("g_hi"), sem("g_lo")
    y_done = sem("y_done")
    y_out = sem("y_out")
    y_ready = sem("y_ready")
    added = [sem(f"added{n}") for n in range(B + 1)]
    fin_in = [sem(f"fin_in{n}") for n in range(B)]
    fin_step = sem("fin_step")
    fin_var, fin_rstd, fin_done = sem("fin_var"), sem("fin_rstd"), sem("fin_done")
    fin_out = sem("fin_out")

    block = ctx.enter_context(nc.Block())

    @block.sync
    def _(sp):
        def load_w1(e):
            sp.wait_ge(w1_cut, e)
            sp.dma_start(w1_raw[:, :, :], w1_d[e].rearrange("(k p) n -> p k n", p=P)).then_inc(w1_in, 16)

        def load_w2(e):
            sp.wait_ge(w2_cut, e)
            sp.dma_start(w2_raw[:, :, :], w2_d[e].rearrange("(k p) n -> p k n", p=P)).then_inc(w2_in, 16)

        sp.dma_start(b1[:, :, :], b1_d.rearrange("p (e m) -> p e m", e=E)).then_inc(bias_in, 16)
        sp.dma_start(b2[:, :, :], b2_d.rearrange("e c -> (e c)").rearrange("(o n) -> o n", o=1).to_broadcast([P, E * C])).then_inc(bias_in, 16)
        load_w1(1)
        load_w2(1)
        for stage, q, n in expert_steps():
            if stage == "cut1" and q + 1 < E:
                load_w1(q + 1)
            elif stage == "cut2" and q + 1 < E:
                load_w2(q + 1)
            elif stage == "load":
                at = FIN_NO[q]
                sp.wait_ge(added[q], 16 * E)
                sp.wait_ge(added[LEFT], 16 * E)
                if at >= FIN_OWN:
                    sp.wait_ge(w1_cut, E)
                    sp.wait_ge(w2_cut, E)
                sp.dma_start(fin[at], acc_d[q * T:(q + 1) * T, :].rearrange("(t p) n -> p t n", p=P)).then_inc(fin_in[at], 16)
            elif stage == "picked":
                sp.wait_ge(best_ready, 1)
                sp.dma_start(left_f[EARLY:B, :], best_f[:, P:P + 1]).then_inc(left_in, 16)
                sp.dma_start(left_gate[EARLY:B, :], best[:, P:P + 1]).then_inc(left_in, 16)
        sp.wait_ge(fin_out, 16 * B)

    @block.gpsimd
    def _(pool):
        def choice(e, j):
            return left_no[:, e:e + 1] if j == LEFT else tok_no[:, j, e:e + 1]

        def gather(q):
            e, tiles, _ = job(q)
            if q >= TOK_RING:
                pool.wait_ge(tp_done, KC * (q - TOK_RING + 1))
            if LEFT in tiles:
                pool.wait_ge(picked, 2)
            for at, j in enumerate(tiles):
                nc.gpsimd.indirect_dma_start(tok[q % TOK_RING][0:rows_of(j), at, :], None, x1_d[:, :],
                                             bass.IndirectOffsetOnAxis(ap=choice(e, j), axis=0)).then_inc(tok_in[q % TOK_RING], 16)

        nc.gpsimd.iota(base_i[:, :, :], pattern=[[T, LATE], [0, E]], base=EARLY * T, channel_multiplier=0).then_inc(bases, 1)
        nc.gpsimd.iota(lbase_i[:, :], pattern=[[0, E]], base=0, channel_multiplier=T).then_inc(bases, 1)
        nc.gpsimd.memset(half2[:, :], -0.5).then_inc(bases, 1)
        gather(2)
        for stage, q, n in expert_steps():
            if stage == "fetch":
                gather(q)
            elif stage == "up" and q < LO_BY_POOL:
                _, _, cols = job(q)
                at = KH * q + n
                if q >= 2 and n == 0:
                    pool.wait_ge(y_done, 3 * (q - 1))
                pool.wait_ge(g_hi, at + 1)
                nc.gpsimd.tensor_tensor(h_lo[:, q % 2, n, 0:cols], g[:, at % G_RING, 0:cols],
                                        h_hi[:, q % 2, n, 0:cols].bitcast(F32), ALU.subtract).then_inc(g_lo, 1)
            elif stage in ("cut1", "cut2"):
                raw, hi, lo, top, done = ((w1_raw, w1_hi, w1_lo, w1_top, w1_cut) if stage == "cut1" else
                                          (w2_raw, w2_hi, w2_lo, w2_top, w2_cut))
                pool.wait_ge(top, q + 1)
                nc.gpsimd.tensor_tensor(lo[q % 2], raw[:, :, :], hi[q % 2].bitcast(F32), ALU.subtract).then_inc(done, 1)
            elif stage == "down":
                e, tiles, _ = job(q)
                j = tiles[n]
                pool.wait_ge(y_ready, 3 * q + n + 1)
                for other, count in ADDS[q, j].items():
                    if count:
                        pool.wait_ge(added[other], 16 * count)
                nc.gpsimd.indirect_dma_start(acc_d[:, :], bass.IndirectOffsetOnAxis(ap=choice(e, j), axis=0),
                                             y[0:rows_of(j), j, :], None, compute_op=ALU.add).then_inc(added[j], 16)
            elif stage == "norm":
                at = FIN_NO[q]
                pool.wait_ge(bases, 3)
                pool.wait_ge(fin_var, 2 * (at + 1))
                nc.gpsimd.tensor_tensor(rstd2[:, at, :], ve2[:, at, :], half2[:, :], ALU.pow).then_inc(fin_rstd, 1)
                pool.wait_ge(fin_rstd, 2 * at + 1)
                nc.gpsimd.tensor_tensor(shift2[:, at, :], nmean[:, at, :], rstd2[:, at, :], ALU.mult).then_inc(fin_rstd, 1)

    @block.scalar
    def _(act):
        for stage, q, n in expert_steps():
            if stage == "turn":
                _, _, cols = job(q)
                for k in range(KC):
                    act.wait_ge(tp_done, KC * q + k + 1)
                    if q >= TOK_RING:
                        act.wait_ge(h_done, KH * (q - TOK_RING + 1))
                    nc.scalar.activation(tt_hi[:, q % TOK_RING, k, 0:cols], tp_ps[k][:, 0:cols], ACT.Copy).then_inc(tp_hi, 1)
            elif stage == "up":
                e, _, cols = job(q)
                at = KH * q + n
                if at == 0:
                    act.wait_ge(bias_in, 32)
                act.wait_ge(h_done, at + 1)
                if at >= G_RING:
                    act.wait_ge(g_lo, at - G_RING + 1)
                nc.scalar.activation(g[:, at % G_RING, 0:cols], h_ps[at % H_RING][:, 0:cols], ACT.Gelu,
                                     bias=b1[:, e, n:n + 1]).then_inc(g_done, 1)
                if q >= 2 and n == 0:
                    act.wait_ge(y_done, 3 * (q - 1))
                act.wait_ge(g_done, at + 1)
                nc.scalar.activation(h_hi[:, q % 2, n, 0:cols], g[:, at % G_RING, 0:cols], ACT.Copy).then_inc(g_hi, 1)
            elif stage in ("cut1", "cut2"):
                raw, hi, came, done = (w1_raw, w1_hi, w1_in, w1_top) if stage == "cut1" else (w2_raw, w2_hi, w2_in, w2_top)
                if q >= 2 and stage == "cut1":
                    act.wait_ge(h_done, KH * (LAST_JOB[q - 2] + 1))
                elif q >= 2:
                    act.wait_ge(y_done, 3 * (LAST_JOB[q - 2] + 1))
                act.wait_ge(came, 16 * (q + 1))
                nc.scalar.activation(hi[q % 2], raw[:, :, :], ACT.Copy).then_inc(done, 1)
        def store(b, at):
            act.wait_ge(fin_done, TT * (at + 1))
            act.dma_start(out_d[b * T:(b + 1) * T, :].rearrange("(t p) n -> p t n", p=P), fin[at]).then_inc(fin_out, 16)

        for b, at in FIN_NO.items():
            act.wait_ge(fin_rstd, 2 * (at + 1))
            for t in range(TT):
                row = fin[at][:, t, :]
                nc.scalar.activation(row, row, ACT.Identity, bias=shift2[:, at, t:t + 1], scale=rstd2[:, at, t:t + 1]).then_inc(fin_done, 1)
            if at:
                store(last, at - 1)
            last = b
        store(last, B - 1)

    @block.vector
    def _(dve):
        made = [0]

        def link(ins):
            made[0] += 1
            ins.then_inc(dve_step2, 1)
            dve.wait_ge(dve_step2, made[0])

        for stage, q, n in expert_steps():
            if stage == "turn":
                _, _, cols = job(q)
                for k in range(KC):
                    dve.wait_ge(tp_hi, KC * q + k + 1)
                    nc.vector.tensor_tensor(tt_lo[:, q % TOK_RING, k, 0:cols], tp_ps[k][:, 0:cols],
                                            tt_hi[:, q % TOK_RING, k, 0:cols].bitcast(F32), ALU.subtract).then_inc(tp_lo, 1)
            elif stage == "round":
                if n == 0:
                    dve.wait_ge(rows_ready, 1)
                    nc.vector.tensor_copy(row_pool[0][:, :], pick_ps[0:late, :]).then_inc(rows_taken, 1)
                    dve.wait_ge(rows_taken, 1)
                pick_round(nc, link, row_pool, best, best_at, n)
                if n == ROUNDS - 1:
                    nc.vector.tensor_copy(best_f[:, :], best_at[:, :]).then_inc(best_ready, 1)
            elif stage == "picked":
                dve.wait_ge(best_t, 1)
                dve.wait_ge(bases, 3)
                src = pick_ps[:, 0:2 * late].rearrange("p (a b e) -> p a b e", a=2, b=LATE)
                link(nc.vector.tensor_copy(gate[:, EARLY:B, :], src[:, 1, :, :]))
                nc.vector.tensor_tensor(tok_no[:, EARLY:B, :], src[:, 0, :, :], base_i[:, :, :], ALU.add).then_inc(picked, 1)
                dve.wait_ge(left_in, 32)
                nc.vector.tensor_tensor(left_no[:, :], left_f[:, :], lbase_i[:, :], ALU.add).then_inc(picked, 1)
            elif stage == "up" and q >= LO_BY_POOL:
                _, _, cols = job(q)
                at = KH * q + n
                if q >= 2 and n == 0:
                    dve.wait_ge(y_done, 3 * (q - 1))
                if q == LO_BY_POOL and n == 0:
                    dve.wait_ge(g_lo, at)
                dve.wait_ge(g_hi, at + 1)
                nc.vector.tensor_tensor(h_lo[:, q % 2, n, 0:cols], g[:, at % G_RING, 0:cols],
                                        h_hi[:, q % 2, n, 0:cols].bitcast(F32), ALU.subtract).then_inc(g_lo, 1)
            elif stage == "down":
                e, tiles, _ = job(q)
                j, at = tiles[n], 3 * q + n
                rows, before = rows_of(j), sum(j in CHUNKS[c] for _, c in JOBS[:q])
                dve.wait_ge(y_done, at + 1)
                if at == 0:
                    dve.wait_ge(bias_in, 32)
                if before:
                    dve.wait_ge(added[j], 16 * before)
                nc.vector.tensor_tensor(y[0:rows, j, :], y_ps[at % Y_RING][0:rows, 0:C], b2[0:rows, e, :], ALU.add).then_inc(y_out, 1)
                dve.wait_ge(y_out, at + 1)
                by = left_gate[:, e:e + 1] if j == LEFT else gate[:, j, e:e + 1]
                nc.vector.tensor_scalar(y[0:rows, j, :], y[0:rows, j, :], by, None, ALU.mult).then_inc(y_ready, 1)
            elif stage == "norm":
                at = FIN_NO[q]
                dve.wait_ge(fin_in[at], 16)
                for t in range(TT):
                    nc.vector.bn_stats(stats2[:, t, :], fin[at][:, t, :]).then_inc(fin_step, 1)
                dve.wait_ge(fin_step, 2 * TT * at + TT)
                for t in range(TT):
                    nc.vector.bn_aggr(mv2[:, at, t, :], stats2[:, t, :]).then_inc(fin_step, 1)
                dve.wait_ge(fin_step, 2 * TT * (at + 1))
                nc.vector.tensor_scalar_add(ve2[:, at, :], mv2[:, at, :, 1], EPS).then_inc(fin_var, 1)
                nc.vector.tensor_scalar_mul(nmean[:, at, :], mv2[:, at, :, 0], -1.0).then_inc(fin_var, 1)

    @block.tensor
    def _(pe):
        for stage, q, n in expert_steps():
            e, tiles, cols = job(q) if stage in ("turn", "up", "down") else (0, (), 0)
            if stage == "turn":
                pe.wait_ge(tok_in[q % TOK_RING], 48 * (q // TOK_RING + 1))
                for k in range(KC):
                    if q:
                        pe.wait_ge(tp_lo, KC * (q - 1) + k + 1)
                    for at, j in enumerate(tiles):
                        rows = rows_of(j)
                        ins = nc.tensor.transpose(tp_ps[k][:, at * P:at * P + rows], tok[q % TOK_RING][0:rows, at, k * P:(k + 1) * P],
                                                  ident[0:rows, 0:rows])
                    ins.then_inc(tp_done, 1)
            elif stage == "rows":
                for t in range(TT):
                    ins = nc.tensor.transpose(pick_ps[0:late, t * P:(t + 1) * P], scores[:, t, EARLY:B, :].rearrange("p b e -> p (b e)"),
                                              ident[:, :])
                ins.then_inc(rows_ready, 1)
            elif stage == "picked":
                pe.wait_ge(best_ready, 1)
                nc.tensor.transpose(pick_ps[:, 0:late], best_f[:, 0:P], ident[0:late, 0:late])
                nc.tensor.transpose(pick_ps[:, late:2 * late], best[:, 0:P], ident[0:late, 0:late]).then_inc(best_t, 1)
            elif stage == "up":
                at = KH * q + n
                if n == 0:
                    pe.wait_ge(tp_hi, KC * (q + 1))
                    pe.wait_ge(tp_lo, KC * (q + 1))
                    pe.wait_ge(w1_cut, e + 1)
                if at >= H_RING:
                    pe.wait_ge(g_done, at - H_RING + 1)
                units = slice(n * P, (n + 1) * P)
                terms = [(w, x, k) for w, x in ((w1_hi, tt_hi), (w1_hi, tt_lo), (w1_lo, tt_hi)) for k in range(KC)]
                for i, (w, x, k) in enumerate(terms):
                    ins = nc.tensor.matmul(h_ps[at % H_RING][:, 0:cols], w[e % 2][:, k, units], x[:, q % TOK_RING, k, 0:cols],
                                           start=i == 0, stop=i == len(terms) - 1)
                ins.then_inc(h_done, 1)
            elif stage == "down":
                at, rows = 3 * q + n, rows_of(tiles[n])
                if n == 0:
                    pe.wait_ge(g_hi, KH * (q + 1))
                    pe.wait_ge(g_lo, KH * (q + 1))
                    pe.wait_ge(w2_cut, e + 1)
                if at >= Y_RING:
                    pe.wait_ge(y_out, at - Y_RING + 1)
                toks = slice(n * P, n * P + rows)
                terms = [(x, w, m) for m in range(KH) for x, w in ((h_hi, w2_hi), (h_lo, w2_hi), (h_hi, w2_lo))]
                for i, (x, w, m) in enumerate(terms):
                    ins = nc.tensor.matmul(y_ps[at % Y_RING][0:rows, 0:C], x[:, q % 2, m, toks], w[e % 2][:, m, :],
                                           start=i == 0, stop=i == len(terms) - 1)
                ins.then_inc(y_done, 1)


def build(nc, xt_d, x_d, wqkv_d, wp_d, rw_d, w1_d, b1_d, w2_d, b2_d, out_d):
    x1_d = nc.dram_tensor("x1", [B * T, C], F32).ap()
    acc_d = nc.dram_tensor("acc", [B * T, C], F32).ap()
    with ExitStack() as both:
        def sb(name, shape, dt):
            return both.enter_context(nc.sbuf_tensor(name, shape, dt))

        ident = sb("ident", [P, P], F32)
        scores = sb("scores", [P, TT, B, E], F32)
        chosen = {
            "tok_no": sb("tok_no", [P, B, E], U32),
            "gate": sb("gate", [P, B, E], F32),
            "left_f": sb("left_f", [B, E], F32),
            "left_gate": sb("left_gate", [B, E], F32),
        }
        ahead = {
            "w1_raw": sb("w1_raw", [P, KC, HID], F32),
            "w2_raw": sb("w2_raw", [P, KH, C], F32),
            "tok0": sb("tok0", [P, 3, C], F32),
            "tok1": sb("tok1", [P, 3, C], F32),
            "w1": sb("w1_parts", [P, 2, 2 * KC * HID], F32),
            "w2": sb("w2_parts", [P, 2, 2 * KH * C], F32),
            "w1_top": both.enter_context(nc.semaphore("w1_top")),
            "w2_top": both.enter_context(nc.semaphore("w2_top")),
            "w1_cut": both.enter_context(nc.semaphore("w1_cut")),
            "w2_cut": both.enter_context(nc.semaphore("w2_cut")),
            "w1_in": both.enter_context(nc.semaphore("w1_in")),
            "w2_in": both.enter_context(nc.semaphore("w2_in")),
            "tok_in0": both.enter_context(nc.semaphore("tok_in0")),
            "tok_in1": both.enter_context(nc.semaphore("tok_in1")),
        }
        with ExitStack() as ctx:
            attention(nc, ctx, xt_d, x_d, wqkv_d, wp_d, rw_d, x1_d, acc_d, ident, scores, chosen, w1_d, w2_d, ahead)
        with ExitStack() as ctx:
            experts(nc, ctx, x1_d, acc_d, w1_d, b1_d, w2_d, b2_d, out_d, ident, scores, chosen, ahead)


def kernel(L0_attn_x, L0_attn_W_key, L0_attn_W_query, L0_attn_W_value, L0_attn_W_proj,
           L0_ffn_router_w, L0_ffn_w1, L0_ffn_b1, L0_ffn_w2, L0_ffn_b2):
    import concourse.bacc as bacc
    from concourse.bass_utils import run_bass_kernel_spmd

    x = np.asarray(L0_attn_x).reshape(B * T, C)
    wqkv = np.concatenate([np.asarray(L0_attn_W_query).T, np.asarray(L0_attn_W_key).T, np.asarray(L0_attn_W_value).T], axis=1)
    arrays = {
        "in_xt": x.T,
        "in_x": x,
        "in_wqkv": wqkv,
        "in_wp": np.asarray(L0_attn_W_proj).T,
        "in_rw": np.asarray(L0_ffn_router_w).T,
        "in_w1": np.asarray(L0_ffn_w1),
        "in_b1": np.asarray(L0_ffn_b1).reshape(E, KH, P).transpose(2, 0, 1).reshape(P, E * KH),
        "in_w2": np.asarray(L0_ffn_w2),
        "in_b2": np.asarray(L0_ffn_b2),
    }
    arrays = {n: np.ascontiguousarray(a) for n, a in arrays.items()}
    nc = bacc.Bacc("TRN2", target_bir_lowering=False, num_devices=1)
    args = [nc.dram_tensor(n, a.shape, mybir.dt.from_np(a.dtype), kind="ExternalInput").ap() for n, a in arrays.items()]
    out = nc.dram_tensor("out_0", (B * T, C), F32, kind="ExternalOutput").ap()
    build(nc, *args, out)
    r = run_bass_kernel_spmd(nc, [arrays], core_ids=[0])
    return r.results[0]["out_0"].reshape(B, T, C)
```
